# Optimizing a Trainium2 kernel written in Bass

```python
import numpy as np
import jax
import jax.numpy as jnp

def _softmax(x, axis=-1):
    return jax.nn.softmax(x, axis=axis)

def _gelu(x):
    return jax.nn.gelu(x, approximate=True)

def _silu(x):
    return jax.nn.silu(x)

def _sigmoid(x):
    return jax.nn.sigmoid(x)

def _layernorm(x, axis=-1, eps=1e-05):
    m = jnp.mean(x, axis=axis, keepdims=True)
    v = jnp.var(x, axis=axis, keepdims=True)
    return (x - m) / jnp.sqrt(v + eps)

def _scatter_add(tgt, idx, src, axis=0):
    return tgt.at[idx].add(src)

def _segment_sum(src, seg, n):
    return jax.ops.segment_sum(src, seg, n)
kernel_name = 'mk_adj_preln_d1_adj_r2_001c57'

def setup_inputs(seed: int=0):
    np.random.seed(seed)
    _w = jnp.asarray

    def _rec_inputs():
        import jax
        import jax.numpy as jnp
        _gk = jax.random.key(seed)
        x = 7.22e-05 + 1 * jax.random.normal(jax.random.fold_in(_gk, 1), (32, 256, 1024), jnp.float32)
        _a = jax.random.bernoulli(jax.random.fold_in(_gk, 2), 0.03125, (256, 256))
        _a = jnp.logical_or(_a, jnp.swapaxes(_a, -1, -2))
        _a = jnp.logical_or(_a, jnp.eye(256, dtype=bool))
        _af = _a.astype(jnp.float32)
        _af = _af * jax.random.uniform(jax.random.fold_in(_gk, 3), (256, 256), jnp.float32, 0.05, 0.0885215)
        adj = _af
        return (x, adj)
    x, adj = _rec_inputs()

    def _L0_gnn_setup():
        import jax, jax.numpy as jnp
        import numpy as np
        B, S, N = (8, 256, 1024)
        HID = 256
        K = 8

        def _construct_adj(x, k):
            Bn, Sn, Nn = x.shape
            fv = x.mean(axis=1)
            nf = fv / jnp.linalg.norm(fv, axis=1, keepdims=True)
            sim = nf[:, :, None] * nf[:, None, :]
            kk = min(k, Nn - 1)
            _, idx = jax.lax.top_k(sim, kk + 1)
            idx = idx[..., 1:]
            b_ix = jnp.arange(Bn)[:, None, None]
            r_ix = jnp.arange(Nn)[None, :, None]
            adj = jnp.zeros((Bn, Nn, Nn), x.dtype).at[b_ix, r_ix, idx].set(1.0)
            adj = jnp.maximum(adj, jnp.swapaxes(adj, 1, 2))
            d = jnp.arange(Nn)
            adj = adj.at[:, d, d].set(1.0)
            return adj

        def _gc(x, adj, W, b):
            deg = adj.sum(axis=2, keepdims=True)
            deg = jnp.where(deg == 0, jnp.ones_like(deg), deg)
            h = x @ W.T + b
            return jnp.einsum('bij,bjh->bih', adj / deg, h)
        key = jax.random.key(seed)
        k0, k1, k2 = jax.random.split(key, 3)
        x = jax.random.normal(k0, (B, S, N), jnp.float32)
        W1 = jax.random.normal(k1, (HID, S), jnp.float32) * 0.02
        b1 = jnp.zeros((HID,), jnp.float32)
        W2 = jax.random.normal(k2, (S, HID), jnp.float32) * 0.02
        b2 = jnp.zeros((S,), jnp.float32)
        return {'x': x, 'W1': W1, 'b1': b1, 'W2': W2, 'b2': b2}
    _L0_gnn_all = _L0_gnn_setup()
    _L0_gnn_in = {k: v for k, v in _L0_gnn_all.items() if k in ('b1', 'b2')}
    del _L0_gnn_all
    return {'x': x, 'adj': adj, 'L0_gnn_b1': _L0_gnn_in['b1'], 'L0_gnn_b2': _L0_gnn_in['b2']}

def reference(x, adj, L0_gnn_b1, L0_gnn_b2):
    import jax
    import jax.numpy as jnp

    def _L0_gnn_ref(x, W1, b1, W2, b2):
        import jax, jax.numpy as jnp
        import numpy as np
        B, S, N = (8, 256, 1024)
        HID = 256
        K = 8

        def _construct_adj(x, k):
            Bn, Sn, Nn = x.shape
            fv = x.mean(axis=1)
            nf = fv / jnp.linalg.norm(fv, axis=1, keepdims=True)
            sim = nf[:, :, None] * nf[:, None, :]
            kk = min(k, Nn - 1)
            _, idx = jax.lax.top_k(sim, kk + 1)
            idx = idx[..., 1:]
            b_ix = jnp.arange(Bn)[:, None, None]
            r_ix = jnp.arange(Nn)[None, :, None]
            adj = jnp.zeros((Bn, Nn, Nn), x.dtype).at[b_ix, r_ix, idx].set(1.0)
            adj = jnp.maximum(adj, jnp.swapaxes(adj, 1, 2))
            d = jnp.arange(Nn)
            adj = adj.at[:, d, d].set(1.0)
            return adj

        def _gc(x, adj, W, b):
            deg = adj.sum(axis=2, keepdims=True)
            deg = jnp.where(deg == 0, jnp.ones_like(deg), deg)
            h = x @ W.T + b
            return jnp.einsum('bij,bjh->bih', adj / deg, h)
        adj = _construct_adj(x, K)
        xr = jnp.swapaxes(x, 1, 2)
        h = jax.nn.relu(_gc(xr, adj, W1, b1))
        h = _gc(h, adj, W2, b2)
        return jnp.swapaxes(h, 1, 2)
    h = jnp.maximum(_layernorm(x, axis=-1), 0.0)
    x = x + _L0_gnn_ref(h, adj, L0_gnn_b1, adj, L0_gnn_b2)
    return x

_drawn_inputs = setup_inputs


def setup_inputs(seed=0):
    import zlib

    import numpy as np

    out = dict(_drawn_inputs(seed))
    spreads = {'L0_gnn_b1': (0.0, 0.341), 'L0_gnn_b2': (0.0, 0.1)}
    factors = {}
    for name, (base, spread) in spreads.items():
        noise = np.random.default_rng([zlib.crc32(name.encode()), seed]).standard_normal(out[name].shape)
        drawn = base * np.exp(spread * noise) if base else spread * noise
        out[name] = jnp.asarray(drawn.astype(out[name].dtype))
    for name, factor in factors.items():
        out[name] = (out[name] * factor).astype(out[name].dtype)
    return out
```

```python
from contextlib import ExitStack

import numpy as np

import concourse.bass as bass
from concourse import mybir

F32 = mybir.dt.float32
F32R = mybir.dt.float32r
BF16 = mybir.dt.bfloat16
ALU = mybir.AluOpType
ACT = mybir.ActivationFunctionType
AX_X = mybir.AxisListType.X

P = 128
KF = 2
N = 1024
H = 512
G = 4
RING = 8
LEAD = 6
K_TOP = 8
NCLS = 8
T_MARK = -1e-30
M_MARK = -4.0
PAST = -5.0
BIG = -(2.0 ** 120)
C_COMMON, C_STATIC = 4, 6
D0 = float(K_TOP + 1)



def class_tables():
    bits = [(c & 1, 1 - (c >> 2), (c >> 1) & 1) for c in range(NCLS)]
    pick = np.array([[(1 - zc) * ms + zc * es for _, ms, es in bits] for zc, _, _ in bits], np.float32)
    adj = np.maximum(pick, pick.T)
    own = 1.0 - np.diag(adj)
    return adj, own


COLS = {}


def constants():
    adj, own = class_tables()
    keep_own = np.diag(np.where(np.isin(np.arange(NCLS), (C_COMMON, C_STATIC)), 0.0, own))
    row = np.arange(P) % 32
    parts = [
        ("cls", np.where(row < 16, row % 8, -1.0)[:, None]),
        ("lo", np.where((row >= 8) & (row < 16), -1.0, 0.0)[:, None]),
        ("eps", np.full((P, 1), 1e-5)),
        ("adj", np.tile(adj.reshape(1, -1), (P, 1))),
        ("keep_own", np.tile(keep_own.reshape(1, -1), (P, 1))),
        ("own", np.tile(own[None], (P, 1))),
        ("adj_common", np.tile(adj[None, :, C_COMMON] * D0, (P, 1))),
        ("adj_static", np.tile(adj[None, :, C_STATIC], (P, 1))),
        ("pick_n", np.array([[float(p % 32 < NCLS and (p // 32) * NCLS + p % 32 == q) for q in range(G * NCLS)]
                             for p in range(P)])),
        ("ones", np.ones((P, P))),
        ("col", np.tile((np.arange(2 * P - 1) == P - 1)[None], (P, 1))),
    ]
    at = 0
    for name, a in parts:
        COLS[name] = (at, at + a.shape[1])
        at += a.shape[1]
    small = np.concatenate([a for _, a in parts], 1).astype(np.float32)
    mask = np.zeros((P, G, P), np.float32)
    spread = np.zeros((P, G + 1, P), np.float32)
    for j in range(G):
        for c in range(NCLS):
            if c not in (C_COMMON, C_STATIC):
                mask[32 * j + c, j] = BIG
        spread[j, j] = 1.0
        spread[j, G, 32 * j:32 * j + 32] = 1.0
    staged = np.concatenate([mask.reshape(P, -1), spread.reshape(P, -1)], 1)
    return small, staged


def build(nc, x, w_t, b1, b2, small, staged, out):
    NB = x.shape[0]
    LOOPS = NB // RING - 1
    S_WID, T_WID = small.shape[1], staged.shape[1]

    with ExitStack() as ctx:
        def sb(name, shape, dt=F32):
            return ctx.enter_context(nc.sbuf_tensor(name, shape, dt))

        def pb(name, shape, dt=F32):
            return ctx.enter_context(nc.psum_tensor(name, shape, dt))

        def sem(name):
            return ctx.enter_context(nc.semaphore(name))

        xb = sb("xb", [P, RING, KF, N])
        hb = sb("hb", [P, RING, KF, N])
        h_hi = sb("h_hi", [P, KF, N], F32R)
        h_lo = sb("h_lo", [P, KF, N], F32R)
        r = sb("r", [P, KF, N])
        r_hi = sb("r_hi", [P, KF, N], F32R)
        r_lo = sb("r_lo", [P, KF, N], F32R)
        hsum = sb("hsum", [P, N])
        fv = sb("fv", [G, N + 8])
        code = sb("code", [P, N], BF16)
        onehot = sb("onehot", [P, 2, N], F32R)
        junk = sb("junk", [P, N], BF16)
        cell = sb("cell", [1, 1])
        w = sb("w", [P, KF, KF * P])
        w_hi = sb("w_hi", [P, KF, KF * P], F32R)
        w_lo = sb("w_lo", [P, KF, KF * P], F32R)
        cst = sb("cst", [P, S_WID])
        mask = sb("mask", [P, G, P], F32R)
        spread = sb("spread", [P, G + 1, P], BF16)
        bias1 = sb("bias1", [P, KF])
        bias2 = sb("bias2", [P, KF])
        stats = sb("stats", [P, KF, 2, 6])
        mv = sb("mv", [P, KF, 2])
        std = sb("std", [P, KF])
        rstd = sb("rstd", [P, 2, KF])
        nmean = sb("nmean", [P, 2, KF])
        h_tot = sb("h_tot", [P, RING, KF])
        h_top = sb("h_top", [P, 2, KF])
        h_sta = sb("h_sta", [P, 2, KF])
        best = sb("best", [G, 8])
        first = sb("first", [G, 8])
        cnt = sb("cnt", [P, 1])
        cnt_d = sb("cnt_d", [P, G * NCLS])
        cnt_b = sb("cnt_b", [P, G, NCLS])
        mix = sb("mix", [P, 2, G, NCLS, NCLS])
        deg = sb("deg", [P, G, NCLS])
        rdeg = sb("rdeg", [P, 2, G, NCLS])
        rdeg2 = sb("rdeg2", [P, 2, G])
        src1 = sb("src1", [P, KF, NCLS])
        pre = sb("pre", [P, KF, NCLS])
        src2 = sb("src2", [P, 2, KF, NCLS])
        beta = sb("beta", [P, 2, KF, 2])
        acc = sb("acc", [P, KF, 3])
        prod = sb("prod", [P, KF, NCLS, NCLS])
        src3 = sb("src3", [P, KF, 96 + P])
        v_hi = sb("v_hi", [P, KF * P], F32R)
        tab = sb("tab", [P, KF * P], F32R)

        ps = [pb(f"ps{u}", [P, H]) for u in range(4)]
        ps_fv = pb("ps_fv", [P, N])
        ps_c = pb("ps_c", [P, N])
        V2 = ps_c[:, 0:KF * P]
        X1 = ps_c[:, KF * P:KF * P + KF * NCLS].rearrange("p (m c) -> p m c", m=KF)
        NBC = ps_c[:, H - G * NCLS:H]

        def c_(name):
            a, b = COLS[name]
            return cst[:, a:b]

        x_loaded = [sem(f"x_loaded{i}") for i in range(RING)]
        x_stored = [sem(f"x_stored{i}") for i in range(RING)]
        consts_loaded = sem("consts_loaded")
        zeroed = sem("zeroed")
        consts_ready = sem("consts_ready")
        stats_ready = sem("stats_ready")
        std_ready = sem("std_ready")
        norm_ready = sem("norm_ready")
        h_ready = sem("h_ready")
        hsum_ready = sem("hsum_ready")
        fv_done = sem("fv_done")
        fv_copied = sem("fv_copied")
        code_ready = sem("code_ready")
        spread_done = sem("spread_done")
        onehot_ready = sem("onehot_ready")
        cntd_ready = sem("cntd_ready")
        cnt_done = sem("cnt_done")
        cnt_copied = sem("cnt_copied")
        mixn_ready = sem("mixn_ready")
        deg_ready = sem("deg_ready")
        mix_ready = sem("mix_ready")
        cls_done = sem("cls_done")
        sums_ready = sem("sums_ready")
        src1_ready = sem("src1_ready")
        x1_done = sem("x1_done")
        beta_ready = sem("beta_ready")
        hhi_ready = sem("hhi_ready")
        hlo_ready = sem("hlo_ready")
        l1_done = sem("l1_done")
        r_ready = sem("r_ready")
        rhi_ready = sem("rhi_ready")
        rlo_ready = sem("rlo_ready")
        src3_ready = sem("src3_ready")
        v2_done = sem("v2_done")
        tab_ready = sem("tab_ready")
        l2_done = sem("l2_done")
        out_ready = sem("out_ready")
        dve_stats = sem("dve_stats")
        dve_rstd = sem("dve_rstd")
        dve_top = sem("dve_top")
        dve_pre = sem("dve_pre")
        dve_acc = sem("dve_acc")
        dve_prod = sem("dve_prod")
        dve_vhi = sem("dve_vhi")
        dve_deg = sem("dve_deg")
        dve_group = sem("dve_group")
        pool_group = sem("pool_group")
        dve_init = sem("dve_init")

        block = ctx.enter_context(nc.Block())

        def slots(eng, slot):
            if LOOPS > 1:
                with eng.Fori(0, LOOPS, 1) as it:
                    for j in range(RING):
                        slot(it, j, False)
            else:
                for it in range(LOOPS):
                    for j in range(RING):
                        slot(it, j, False)
            for j in range(RING):
                slot(LOOPS, j, True)

        def at(it, j, per, k):
            return it * (RING * per) + (per * j + k)

        def at_group(it, j, per, k):
            return it * (RING // G * per) + (per * (j // G) + k)

        @block.sync
        def _(sp):
            sp.dma_start(xb[:, 0], x[0].rearrange("(k p) n -> p k n", p=P)).then_inc(x_loaded[0], 16)
            sp.dma_start(cst[:], small).then_inc(consts_loaded, 16)
            sp.dma_start(r[:].rearrange("p k n -> p (k n)")[:, 0:T_WID], staged).then_inc(consts_loaded, 16)
            sp.dma_start(w[:], w_t.rearrange("(k p) n -> p k n", p=P)).then_inc(consts_loaded, 16)
            sp.dma_start(bias1[:], b1).then_inc(consts_loaded, 16)
            sp.dma_start(bias2[:], b2).then_inc(consts_loaded, 16)
            for b in range(1, RING):
                sp.dma_start(xb[:, b], x[b].rearrange("(k p) n -> p k n", p=P)).then_inc(x_loaded[b], 16)

            x_all = x.rearrange("b (k p) n -> p b k n", p=P)
            out_all = out.rearrange("b (k p) n -> p b k n", p=P)

            def slot(it, j, last):
                b = it * RING + j
                sp.wait_ge(out_ready, at(it, j, 4, 8))
                src = xb[:, j:j + 1]
                dst = out_all[:, b:b + 1] if isinstance(b, int) else out_all[:, bass.ds(b, 1)]
                sp.dma_start(dst, src).then_inc(x_stored[j], 16)
                if not last:
                    sp.wait_ge(x_stored[j], it * 16 + 16)
                    nb = it * RING + (j + RING)
                    nxt = x_all[:, nb:nb + 1] if isinstance(nb, int) else x_all[:, bass.ds(nb, 1)]
                    sp.dma_start(xb[:, j:j + 1], nxt).then_inc(x_loaded[j], 16)

            slots(sp, slot)
            for j in range(RING):
                sp.wait_ge(x_stored[j], 16 * (NB // RING))

        @block.scalar
        def _(act):
            def normalise(it, j, k):
                a = (j + k) % RING
                act.wait_ge(stats_ready, at(it, j, 1, k + 1))
                nc.scalar.activation(std[:], mv[:, :, 1], ACT.Sqrt,
                                     bias=c_("eps")).then_inc(std_ready, 1)
                act.wait_ge(norm_ready, at(it, j, 1, k + 1))
                for kf in range(KF):
                    last = nc.scalar.activation(
                        hb[:, a, kf], xb[:, a, kf], ACT.Relu, bias=nmean[:, a % 2, kf:kf + 1],
                        scale=rstd[:, a % 2, kf:kf + 1], accum_out=h_tot[:, a, kf:kf + 1])
                last.then_inc(h_ready, 1)

            def split_h(it, j, k, half):
                a = (j + k) % RING
                n = slice(half * H, half * H + H)
                nc.scalar.activation(h_hi[:, :, n], hb[:, a, :, n], ACT.Copy).then_inc(hhi_ready, 1)

            def relu(it, j, half, m):
                u = 2 * half + m
                par = j % 2
                act.wait_ge(l1_done, at(it, j, 4, u + 1))
                if u == 0:
                    act.wait_ge(beta_ready, at(it, j, 1, 1))
                com = dict(bias=beta[:, par, m, 0:1], scale=1.0 / (D0 * D0))
                if half == 0:
                    nc.scalar.activation(r[:, m, K_TOP + 1:H], ps[u][:, K_TOP + 1:H], ACT.Relu,
                                         accum_out=acc[:, m, 0:1], **com)
                    nc.scalar.activation(r[:, m, 0:1], ps[u][:, 0:1], ACT.Relu,
                                         accum_out=acc[:, m, 1:2], **com)
                    last = nc.scalar.activation(
                        r[:, m, 1:K_TOP + 1], ps[u][:, 1:K_TOP + 1], ACT.Relu, bias=beta[:, par, m, 1:2],
                        scale=rdeg2[:, (j // G) % 2, j % G:j % G + 1],
                        accum_out=src2[:, par, m, C_STATIC:C_STATIC + 1])
                else:
                    last = nc.scalar.activation(r[:, m, H:N], ps[u][:], ACT.Relu,
                                                accum_out=acc[:, m, 2:3], **com)
                last.then_inc(r_ready, 1)

            def split_r(it, j, half):
                act.wait_ge(r_ready, at(it, j, 4, 2 * half + 2))
                n = slice(half * H, half * H + H)
                nc.scalar.activation(r_hi[:, :, n], r[:, :, n], ACT.Copy).then_inc(rhi_ready, 1)

            act.wait_ge(consts_ready, 1)
            for a in range(LEAD):
                normalise(0, 0, a)
                if a == 0:
                    act.wait_ge(h_ready, 1)
                    split_h(0, 0, 0, 0)
                    split_h(0, 0, 0, 1)

            def slot(it, j, last):
                relu(it, j, 0, 0)
                relu(it, j, 0, 1)
                split_r(it, j, 0)
                relu(it, j, 1, 0)
                relu(it, j, 1, 1)
                split_r(it, j, 1)
                more = not (last and j == RING - 1)
                if more:
                    split_h(it, j, 1, 0)
                if not (last and j >= RING - LEAD):
                    normalise(it, j, LEAD)
                if more:
                    split_h(it, j, 1, 1)

            slots(act, slot)

        @block.gpsimd
        def _(pool):
            def sum_chunks(it, j, k):
                a = (j + k) % RING
                pool.wait_ge(h_ready, at(it, j, 1, k + 1))
                if not (isinstance(it, int) and it == 0 and j + k == 0):
                    pool.wait_ge(fv_done, at(it, j, 1, k))
                nc.gpsimd.tensor_tensor(hsum[:], hb[:, a, 0], hb[:, a, 1], ALU.add).then_inc(hsum_ready, 1)

            def split_h(it, j, k, half):
                a = (j + k) % RING
                n = slice(half * H, half * H + H)
                pool.wait_ge(hhi_ready, at(it, j, 2, 2 * k + half + 1))
                nc.gpsimd.tensor_tensor(h_lo[:, :, n], hb[:, a, :, n], h_hi[:, :, n].bitcast(F32),
                                        ALU.subtract).then_inc(hlo_ready, 1)

            def sources(it, j, k):
                t = j + k
                a, par, gp, g = t % RING, t % 2, (t // G) % 2, t % G
                rd = rdeg[:, gp, g]
                pool.wait_ge(sums_ready, at(it, j, 1, k + 1))
                if t % G == 0:
                    pool.wait_ge(deg_ready, at_group(it, t, 1, 1))
                for c, sums in ((slice(0, 4), h_tot[:, a]), (slice(4, 8, 2), h_top[:, par]),
                                (slice(5, 8, 2), h_sta[:, par])):
                    n = len(range(*c.indices(NCLS)))
                    last = nc.gpsimd.tensor_tensor(
                        src1[:, :, c], rd[:, c].unsqueeze(1).broadcast_to([P, KF, n]),
                        sums.unsqueeze(2).broadcast_to([P, KF, n]), ALU.mult)
                last.then_inc(src1_ready, 1)

            def tables(it, j, k):
                t = j + k
                gp = (t // G) % 2
                mx = mix[:, gp]
                pool.wait_ge(cnt_copied, at_group(it, t, 1, 1))
                shape = [P, G, NCLS, NCLS]
                nc.gpsimd.tensor_tensor(
                    mx, c_("adj").rearrange("p (c s) -> p c s", c=NCLS).unsqueeze(1).broadcast_to(shape),
                    cnt_b[:].unsqueeze(2).broadcast_to(shape), ALU.mult).then_inc(mixn_ready, 1)
                pool.wait_ge(deg_ready, at_group(it, t, 1, 1))
                nc.gpsimd.tensor_tensor(rdeg2[:, gp], rdeg[:, gp, :, C_STATIC], rdeg[:, gp, :, C_STATIC], ALU.mult)
                nc.gpsimd.tensor_copy(mx[:, :, :, C_COMMON],
                                      c_("adj_common").unsqueeze(1).broadcast_to([P, G, NCLS]))
                nc.gpsimd.tensor_tensor(
                    mx[:, :, :, C_STATIC], c_("adj_static").unsqueeze(1).broadcast_to([P, G, NCLS]),
                    deg[:, :, C_STATIC].unsqueeze(2).broadcast_to([P, G, NCLS]),
                    ALU.mult).then_inc(pool_group, 1)
                pool.wait_ge(pool_group, at_group(it, t, 2, 1))
                nc.gpsimd.tensor_tensor(
                    mx, mx, c_("keep_own").rearrange("p (c s) -> p c s", c=NCLS).unsqueeze(1).broadcast_to(shape),
                    ALU.add).then_inc(pool_group, 1)
                pool.wait_ge(pool_group, at_group(it, t, 2, 2))
                nc.gpsimd.tensor_tensor(
                    mx, mx, rdeg[:, gp].unsqueeze(3).broadcast_to(shape), ALU.mult).then_inc(mix_ready, 1)

            pool.wait_ge(consts_ready, 1)
            for a in range(LEAD):
                sum_chunks(0, 0, a)
                if a == 0:
                    split_h(0, 0, 0, 0)
                    split_h(0, 0, 0, 1)
                if a == G - 1:
                    tables(0, 0, 0)
            sources(0, 0, 0)

            def slot(it, j, last):
                more = not (last and j == RING - 1)
                if more:
                    sources(it, j, 1)
                    split_h(it, j, 1, 0)
                    split_h(it, j, 1, 1)
                if not (last and j >= RING - LEAD):
                    sum_chunks(it, j, LEAD)
                if j % G == 2 and not (last and j >= G):
                    tables(it, j, 2)

            slots(pool, slot)

        @block.tensor
        def _(pe):
            def column_sums(it, j, k):
                t = j + k
                pe.wait_ge(hsum_ready, at(it, j, 1, k + 1))
                if t % G == 0 and not (isinstance(it, int) and it == 0 and t == 0):
                    pe.wait_ge(fv_copied, at_group(it, t, 1, 0))
                a, _ = COLS["col"]
                col = cst[:, a + P - 1 - t % G:a + 2 * P - 1 - t % G]
                for half in range(2):
                    n = slice(half * H, half * H + H)
                    last = nc.tensor.matmul(ps_fv[:, n], col, hsum[:, n], start=(t % G == 0),
                                            stop=(t % G == G - 1), skip_group_check=True)
                last.then_inc(fv_done, 1)

            def spread_group(it, j, k):
                t = j + k
                pe.wait_ge(code_ready, at_group(it, t, 1, 1))
                for half in range(2):
                    n = slice(half * H, half * H + H)
                    last = nc.tensor.matmul(ps_c[:, n], spread[:, G], code[:, n], start=True, stop=True)
                last.then_inc(spread_done, 1)
                pe.wait_ge(cntd_ready, at_group(it, t, 1, 1))
                nc.tensor.matmul(NBC, c_("ones"), cnt_d[:], start=True, stop=True).then_inc(cnt_done, 1)

            def spread_batch(it, j, k):
                t = j + k
                if t % G == 0:
                    pe.wait_ge(cnt_copied, at_group(it, t, 1, 1))
                for half in range(2):
                    n = slice(half * H, half * H + H)
                    last = nc.tensor.matmul(ps_c[:, n], spread[:, t % G], code[:, n], start=True, stop=True)
                last.then_inc(cls_done, 1)

            def class_values(it, j, k):
                pe.wait_ge(src1_ready, at(it, j, 1, k + 1))
                pe.wait_ge(sums_ready, at(it, j, 1, k + 1))
                for m in range(KF):
                    for kf in range(KF):
                        last = nc.tensor.matmul(X1[:, m], w[:, kf, m * P:m * P + P], src1[:, kf],
                                                start=(kf == 0), stop=(kf == KF - 1))
                last.then_inc(x1_done, 1)

            def product(u, hi, lo, last_of_group):
                half, m = divmod(u, 2)
                n, mm = slice(half * H, half * H + H), slice(m * P, m * P + P)
                for kf in range(KF):
                    for i, (wt, mov) in enumerate(((w_hi, hi), (w_hi, lo), (w_lo, hi))):
                        nc.tensor.matmul(ps[u][:], wt[:, kf, mm], mov[:, kf, n],
                                         start=(kf == 0 and i == 0), stop=False)

            def layer1(it, j):
                for u in range(4):
                    half, m = divmod(u, 2)
                    n = slice(half * H, half * H + H)
                    if m == 0:
                        pe.wait_ge(hlo_ready, at(it, j, 2, half + 1))
                    pe.wait_ge(out_ready, at(it, j, 4, u + 1))
                    product(u, h_hi, h_lo, False)
                    nc.tensor.matmul(ps[u][:], mask[:, j % G], onehot[:, (j // G) % 2, n],
                                     start=False, stop=True).then_inc(l1_done, 1)

            def layer2(it, j):
                for u in range(4):
                    half, m = divmod(u, 2)
                    if m == 0:
                        pe.wait_ge(rlo_ready, at(it, j, 2, half + 1))
                    product(u, r_hi, r_lo, False)
                    if u == 2:
                        pe.wait_ge(src3_ready, at(it, j, 1, 1))
                        a = 96 - 32 * (j % G)
                        for kf in range(KF):
                            last = nc.tensor.matmul(V2, src3[:, kf, a:a + P], w[:, kf],
                                                    start=(kf == 0), stop=(kf == KF - 1))
                        last.then_inc(v2_done, 1)
                pe.wait_ge(tab_ready, at(it, j, 1, 1))
                for u in range(4):
                    half, m = divmod(u, 2)
                    n = slice(half * H, half * H + H)
                    nc.tensor.matmul(ps[u][:], tab[:, m * P:m * P + P], onehot[:, (j // G) % 2, n],
                                     start=False, stop=True).then_inc(l2_done, 1)

            pe.wait_ge(consts_ready, 1)
            for a in range(G):
                column_sums(0, 0, a)
            spread_group(0, 0, 0)
            spread_batch(0, 0, 0)
            for a in range(G, LEAD):
                column_sums(0, 0, a)
            class_values(0, 0, 0)

            def slot(it, j, last):
                more = not (last and j == RING - 1)
                if more:
                    pe.wait_ge(beta_ready, at(it, j, 1, 1))
                    spread_batch(it, j, 1)
                layer1(it, j)
                if more:
                    class_values(it, j, 1)
                layer2(it, j)
                if not (last and j >= RING - LEAD):
                    column_sums(it, j, LEAD)
                if j % G == 2 and not (last and j >= G):
                    spread_group(it, j, 2)

            slots(pe, slot)

        @block.vector
        def _(dve):
            def hold(s, value):
                dve.wait_ge(s, value)
                nc.vector.memset(cell[:], 0.0)

            def moments(it, j, k):
                a = (j + k) % RING
                q = (j + k) // RING
                dve.wait_ge(x_loaded[a], it * 16 + 16 * (q + 1))
                for kf in range(KF):
                    for half in range(2):
                        last = nc.vector.bn_stats(stats[:, kf, half], xb[:, a, kf, half * H:half * H + H])
                last.then_inc(dve_stats, 1)
                hold(dve_stats, at(it, j, 1, k + 1))
                for kf in range(KF):
                    last = nc.vector.bn_aggr(mv[:, kf], stats[:, kf].rearrange("p a b -> p (a b)"))
                last.then_inc(stats_ready, 1)

            def scales(it, j, k):
                a = (j + k) % RING
                dve.wait_ge(std_ready, at(it, j, 1, k + 1))
                nc.vector.reciprocal(rstd[:, a % 2], std[:]).then_inc(dve_rstd, 1)
                dve.wait_ge(dve_rstd, at(it, j, 1, k + 1))
                nc.vector.scalar_tensor_tensor(nmean[:, a % 2], mv[:, :, 0], -1.0, rstd[:, a % 2],
                                               ALU.mult, ALU.mult).then_inc(norm_ready, 1)

            def node_sums(it, j, k):
                t = j + k
                a, par = t % RING, t % 2
                dve.wait_ge(h_ready, at(it, j, 1, k + 1))
                nc.vector.tensor_reduce(h_sta[:, par], hb[:, a, :, 1:K_TOP + 1], AX_X, ALU.add)
                dve.wait_ge(cls_done, at(it, j, 1, k + 1))
                for kf in range(KF):
                    if kf > 0:
                        dve.wait_ge(dve_top, at(it, j, 1, k + 1))
                    last = nc.vector.scalar_tensor_tensor(junk[:], ps_c[:], 4.0, hb[:, a, kf], ALU.is_lt,
                                                          ALU.mult, accum_out=h_top[:, par, kf:kf + 1])
                    last.then_inc(dve_top if kf == 0 else sums_ready, 1)

            def class_biases(it, j, k):
                t = j + k
                par, gp, g = t % 2, (t // G) % 2, t % G
                dve.wait_ge(x1_done, at(it, j, 1, k + 1))
                nc.vector.tensor_tensor(pre[:], X1, bias1[:].unsqueeze(2).broadcast_to([P, KF, NCLS]),
                                        ALU.add).then_inc(dve_pre, 1)
                dve.wait_ge(dve_pre, at(it, j, 1, k + 1))
                nc.vector.tensor_scalar(src2[:, par], pre[:], 0.0, None, ALU.max)
                nc.vector.tensor_tensor(
                    beta[:, par], pre[:, :, C_COMMON:NCLS:2],
                    rdeg[:, gp, g, C_COMMON:NCLS:2].unsqueeze(1).broadcast_to([P, KF, 2]),
                    ALU.mult).then_inc(beta_ready, 1)

            def split_r(it, j, half):
                n = slice(half * H, half * H + H)
                dve.wait_ge(rhi_ready, at(it, j, 2, half + 1))
                nc.vector.tensor_tensor(r_lo[:, :, n], r[:, :, n], r_hi[:, :, n].bitcast(F32),
                                        ALU.subtract).then_inc(rlo_ready, 1)

            def class_terms(it, j):
                par, gp, g = j % 2, (j // G) % 2, j % G
                dve.wait_ge(r_ready, at(it, j, 4, 4))
                nc.vector.tensor_reduce(src2[:, par, :, C_COMMON], acc[:], AX_X, ALU.add).then_inc(dve_acc, 1)
                if g == 0:
                    dve.wait_ge(mix_ready, at_group(it, j, 1, 1))
                dve.wait_ge(dve_acc, at(it, j, 1, 1))
                for kf in range(KF):
                    last = nc.vector.tensor_tensor(
                        prod[:, kf], src2[:, par, kf].unsqueeze(1).broadcast_to([P, NCLS, NCLS]),
                        mix[:, gp, g], ALU.mult)
                last.then_inc(dve_prod, 1)
                dve.wait_ge(dve_prod, at(it, j, 1, 1))
                for dup in range(2):
                    last = nc.vector.tensor_reduce(src3[:, :, 96 + 8 * dup:104 + 8 * dup], prod[:], AX_X, ALU.add)
                last.then_inc(src3_ready, 1)

            def table(it, j):
                dve.wait_ge(v2_done, at(it, j, 1, 1))
                nc.vector.tensor_copy(v_hi[:], V2).then_inc(dve_vhi, 1)
                dve.wait_ge(dve_vhi, at(it, j, 1, 1))
                nc.vector.scalar_tensor_tensor(tab[:], v_hi[:].bitcast(F32), c_("lo"), V2,
                                               ALU.mult, ALU.add).then_inc(tab_ready, 1)

            def finish(it, j):
                for u in range(4):
                    half, m = divmod(u, 2)
                    n = slice(half * H, half * H + H)
                    dve.wait_ge(l2_done, at(it, j, 4, u + 1))
                    nc.vector.scalar_tensor_tensor(xb[:, j, m, n], ps[u][:], bias2[:, m:m + 1],
                                                   xb[:, j, m, n], ALU.add, ALU.add).then_inc(out_ready, 1)

            def top_nodes(it, j, k):
                t = j + k
                n_step = [0]

                def link(ins):
                    n_step[0] += 1
                    ins.then_inc(dve_group, 1)
                    hold(dve_group, at_group(it, t, TOP_STEPS, n_step[0]))

                dve.wait_ge(fv_done, at(it, j, 1, k + G))
                nc.vector.memset(first[:], PAST)
                nc.vector.memset(fv[:, N:], PAST)
                if not (isinstance(it, int) and it == 0 and t == 0):
                    dve.wait_ge(cls_done, at(it, j, 1, k))
                nc.vector.tensor_scalar(code[0:G], ps_fv[0:G], 0.0, 4.0, ALU.is_equal, ALU.add)
                link(nc.vector.tensor_copy(fv[:, 0:N], ps_fv[0:G]))
                nc.vector.tensor_scalar(code[0:G, 1:K_TOP + 1], code[0:G, 1:K_TOP + 1], 2.0, None,
                                        ALU.add).then_inc(fv_copied, 1)
                link(nc.vector.max(best[:], fv[:, 0:N]))
                link(nc.vector.tensor_copy(first[:, 0:1], best[:, 0:1]))
                link(nc.vector.match_replace(fv[:], first[:], fv[:], T_MARK))
                link(nc.vector.max(best[:], fv[:, 0:N]))
                link(nc.vector.match_replace(fv[:, 0:N], best[:], fv[:, 0:N], M_MARK))
                nc.vector.scalar_tensor_tensor(code[0:G], fv[:, 0:N], 0.0, code[0:G], ALU.min,
                                               ALU.add).then_inc(code_ready, 1)

            def group_tables(it, j, k):
                t = j + k
                gp = (t // G) % 2
                dve.wait_ge(spread_done, at_group(it, t, 1, 1))
                nc.vector.tensor_scalar(onehot[:, gp], ps_c[:], c_("cls"), None, ALU.is_equal, ALU.add,
                                        accum_out=cnt[:]).then_inc(onehot_ready, 1)
                dve.wait_ge(onehot_ready, at_group(it, t, 1, 1))
                nc.vector.tensor_scalar(cnt_d[:], c_("pick_n"), cnt[:], None, ALU.mult).then_inc(cntd_ready, 1)
                dve.wait_ge(cnt_done, at_group(it, t, 1, 1))
                nc.vector.tensor_copy(cnt_b[:].rearrange("p g c -> p (g c)"), NBC).then_inc(cnt_copied, 1)
                dve.wait_ge(mixn_ready, at_group(it, t, 1, 1))
                nc.vector.tensor_reduce(deg[:], mix[:, gp], AX_X, ALU.add).then_inc(dve_deg, 1)
                dve.wait_ge(dve_deg, at_group(it, t, 2, 1))
                nc.vector.tensor_tensor(deg[:], deg[:], c_("own").unsqueeze(1).broadcast_to([P, G, NCLS]),
                                        ALU.add).then_inc(dve_deg, 1)
                dve.wait_ge(dve_deg, at_group(it, t, 2, 2))
                nc.vector.reciprocal(rdeg[:, gp], deg[:]).then_inc(deg_ready, 1)

            TOP_STEPS = 6
            nc.vector.memset(code[:], 0.0).then_inc(zeroed, 1)
            nc.vector.memset(src3[:], 0.0).then_inc(zeroed, 1)
            dve.wait_ge(consts_loaded, 16 * 5)
            flat = r[:].rearrange("p k n -> p (k n)")
            nc.vector.tensor_copy(mask[:].rearrange("p g n -> p (g n)"), flat[:, 0:G * P])
            nc.vector.tensor_copy(spread[:].rearrange("p g n -> p (g n)"), flat[:, G * P:T_WID])
            nc.vector.tensor_copy(w_hi[:], w[:]).then_inc(dve_init, 1)
            dve.wait_ge(dve_init, 1)
            nc.vector.tensor_tensor(w_lo[:], w[:], w_hi[:].bitcast(F32), ALU.subtract).then_inc(out_ready, 4)
            dve.wait_ge(out_ready, 4)
            nc.vector.memset(junk[:], 0.0).then_inc(consts_ready, 1)

            for a in range(G):
                moments(0, 0, a)
                scales(0, 0, a)
            top_nodes(0, 0, 0)
            group_tables(0, 0, 0)
            for a in range(G, LEAD):
                moments(0, 0, a)
                scales(0, 0, a)
            node_sums(0, 0, 0)
            class_biases(0, 0, 0)

            def slot(it, j, last):
                more = not (last and j == RING - 1)
                ahead = not (last and j >= RING - LEAD)
                if more:
                    node_sums(it, j, 1)
                if ahead:
                    moments(it, j, LEAD)
                split_r(it, j, 0)
                if ahead:
                    scales(it, j, LEAD)
                if more:
                    class_biases(it, j, 1)
                split_r(it, j, 1)
                class_terms(it, j)
                table(it, j)
                finish(it, j)
                if j % G == 2 and not (last and j >= G):
                    top_nodes(it, j, 2)
                    group_tables(it, j, 2)

            slots(dve, slot)


def kernel(x, adj, L0_gnn_b1, L0_gnn_b2):
    import concourse.bacc as bacc
    from concourse.bass_utils import run_bass_kernel_spmd

    small, staged = constants()
    arrays = {
        "x": np.ascontiguousarray(x),
        "w_t": np.ascontiguousarray(np.asarray(adj).T),
        "b1": np.ascontiguousarray(np.asarray(L0_gnn_b1).reshape(KF, P).T),
        "b2": np.ascontiguousarray(np.asarray(L0_gnn_b2).reshape(KF, P).T),
        "small": small,
        "staged": staged,
    }
    nc = bacc.Bacc("TRN2", target_bir_lowering=False, num_devices=1)
    ins = [nc.dram_tensor(name, a.shape, F32, kind="ExternalInput").ap() for name, a in arrays.items()]
    out = nc.dram_tensor("out", arrays["x"].shape, F32, kind="ExternalOutput").ap()
    build(nc, *ins, out)
    result = run_bass_kernel_spmd(nc, [arrays], core_ids=[0])
    return result.results[0]["out"]
```

```python
from contextlib import ExitStack

import numpy as np

import concourse.bass as bass
from concourse import mybir

F32 = mybir.dt.float32
F32R = mybir.dt.float32r
BF16 = mybir.dt.bfloat16
ALU = mybir.AluOpType
ACT = mybir.ActivationFunctionType
AX_X = mybir.AxisListType.X

P = 128
KF = 2
N = 1024
H = 512
G = 4
RING = 8
LEAD = 6
K_TOP = 8
NCLS = 8
T_MARK = -1e-30
M_MARK = -4.0
PAST = -5.0
BIG = -(2.0 ** 120)
C_COMMON, C_STATIC = 4, 6
D0 = float(K_TOP + 1)



def class_tables():
    bits = [(c & 1, 1 - (c >> 2), (c >> 1) & 1) for c in range(NCLS)]
    pick = np.array([[(1 - zc) * ms + zc * es for _, ms, es in bits] for zc, _, _ in bits], np.float32)
    adj = np.maximum(pick, pick.T)
    own = 1.0 - np.diag(adj)
    return adj, own


COLS = {}


def constants():
    adj, own = class_tables()
    keep_own = np.diag(np.where(np.isin(np.arange(NCLS), (C_COMMON, C_STATIC)), 0.0, own))
    row = np.arange(P) % 32
    parts = [
        ("cls", np.where(row < 24, row % 8, -1.0)[:, None]),
        ("less_hi", np.where((row >= 8) & (row < 24), -1.0, 0.0)[:, None]),
        ("less_mid", np.where((row >= 16) & (row < 24), -1.0, 0.0)[:, None]),
        ("eps", np.full((P, 1), 1e-5)),
        ("adj", np.tile(adj.reshape(1, -1), (P, 1))),
        ("keep_own", np.tile(keep_own.reshape(1, -1), (P, 1))),
        ("own", np.tile(own[None], (P, 1))),
        ("adj_common", np.tile(adj[None, :, C_COMMON] * D0, (P, 1))),
        ("adj_static", np.tile(adj[None, :, C_STATIC], (P, 1))),
        ("pick_n", np.array([[float(p % 32 < NCLS and (p // 32) * NCLS + p % 32 == q) for q in range(G * NCLS)]
                             for p in range(P)])),
        ("ones", np.ones((P, P))),
    ]
    at = 0
    for name, a in parts:
        COLS[name] = (at, at + a.shape[1])
        at += a.shape[1]
    small = np.concatenate([a for _, a in parts], 1).astype(np.float32)
    mask = np.zeros((P, G, P), np.float32)
    spread = np.zeros((P, G + 1, P), np.float32)
    for j in range(G):
        for c in range(NCLS):
            if c not in (C_COMMON, C_STATIC):
                mask[32 * j + c, j] = BIG
        spread[j, j] = 1.0
        spread[j, G, 32 * j:32 * j + 32] = 1.0
    col = np.tile((np.arange(P + G - 1) == G - 1)[None], (P, 1)).astype(np.float32)
    staged = np.concatenate([mask.reshape(P, -1), spread.reshape(P, -1), col], 1)
    return small, staged


def build(nc, x, w_t, b1, b2, small, staged, out):
    NB = x.shape[0]
    LOOPS = NB // RING - 1
    S_WID, T_WID = small.shape[1], staged.shape[1]

    with ExitStack() as ctx:
        def sb(name, shape, dt=F32):
            return ctx.enter_context(nc.sbuf_tensor(name, shape, dt))

        def pb(name, shape, dt=F32):
            return ctx.enter_context(nc.psum_tensor(name, shape, dt))

        def sem(name):
            return ctx.enter_context(nc.semaphore(name))

        xb = sb("xb", [P, RING, KF, N])
        hb = sb("hb", [P, RING, KF, N])
        h_hi = sb("h_hi", [P, KF, N], F32R)
        h_lo = sb("h_lo", [P, KF, N], F32R)
        r = sb("r", [P, KF, N])
        r_hi = sb("r_hi", [P, KF, N], F32R)
        r_lo = sb("r_lo", [P, KF, N], F32R)
        hsum = sb("hsum", [P, N])
        hsum_hi = sb("hsum_hi", [P, N], F32R)
        hsum_lo = sb("hsum_lo", [P, N], F32R)
        col = sb("col", [P, P + G - 1], F32R)
        fv = sb("fv", [G, N + 8])
        code = sb("code", [P, N], BF16)
        onehot = sb("onehot", [P, 2, N], BF16)
        cell = sb("cell", [1, 1])
        w = sb("w", [P, KF, KF * P])
        w_hi = sb("w_hi", [P, KF, KF * P], F32R)
        w_lo = sb("w_lo", [P, KF, KF * P], F32R)
        cst = sb("cst", [P, S_WID])
        mask = sb("mask", [P, G, P], BF16)
        spread = sb("spread", [P, G + 1, P], BF16)
        bias1 = sb("bias1", [P, KF])
        bias2 = sb("bias2", [P, KF])
        stats = sb("stats", [P, KF, 2, 6])
        mv = sb("mv", [P, KF, 2])
        std = sb("std", [P, KF])
        rstd = sb("rstd", [P, 2, KF])
        nmean = sb("nmean", [P, 2, KF])
        h_tot = sb("h_tot", [P, RING, KF])
        h_top = sb("h_top", [P, 2, KF])
        h_sta = sb("h_sta", [P, 2, KF])
        best = sb("best", [G, 8])
        first = sb("first", [G, 8])
        cnt = sb("cnt", [P, 1])
        cnt_d = sb("cnt_d", [P, G * NCLS])
        cnt_b = sb("cnt_b", [P, G, NCLS])
        mix = sb("mix", [P, 2, G, NCLS, NCLS])
        deg = sb("deg", [P, G, NCLS])
        rdeg = sb("rdeg", [P, 2, G, NCLS])
        rdeg2 = sb("rdeg2", [P, 2, G])
        src1 = sb("src1", [P, KF, NCLS])
        pre = sb("pre", [P, KF, NCLS])
        src2 = sb("src2", [P, 2, KF, NCLS])
        beta = sb("beta", [P, 2, KF, 2])
        acc = sb("acc", [P, KF, 3])
        prod = sb("prod", [P, KF, NCLS, NCLS])
        src3 = sb("src3", [P, KF, 96 + P])
        v_hi = sb("v_hi", [P, KF * P], BF16)
        v_rest = sb("v_rest", [P, KF * P])
        tab = sb("tab", [P, KF * P], BF16)

        ps = [pb(f"ps{u}", [P, H]) for u in range(4)]
        ps_fv = pb("ps_fv", [P, N])
        ps_c = pb("ps_c", [P, N])
        V2 = ps_c[:, H:H + KF * P]
        X1 = ps_c[:, 0:KF * NCLS].rearrange("p (m c) -> p m c", m=KF)
        NBC = ps_c[:, H - G * NCLS:H]

        junk = r_hi[:, :, H:N]

        def c_(name):
            a, b = COLS[name]
            return cst[:, a:b]

        x_loaded = [sem(f"x_loaded{i}") for i in range(RING)]
        x_stored = [sem(f"x_stored{i}") for i in range(RING)]
        consts_loaded = sem("consts_loaded")
        zeroed = sem("zeroed")
        consts_ready = sem("consts_ready")
        stats_ready = sem("stats_ready")
        std_ready = sem("std_ready")
        norm_ready = sem("norm_ready")
        h_ready = sem("h_ready")
        hsum_ready = sem("hsum_ready")
        hshi_ready = sem("hshi_ready")
        hslo_ready = sem("hslo_ready")
        fv_done = sem("fv_done")
        fv_copied = sem("fv_copied")
        zero_ready = sem("zero_ready")
        code_ready = sem("code_ready")
        spread_done = sem("spread_done")
        onehot_ready = sem("onehot_ready")
        cntd_ready = sem("cntd_ready")
        cnt_done = sem("cnt_done")
        cnt_copied = sem("cnt_copied")
        deg_ready = sem("deg_ready")
        mix_ready = sem("mix_ready")
        cls_done = sem("cls_done")
        sums_ready = sem("sums_ready")
        src1_ready = sem("src1_ready")
        x1_done = sem("x1_done")
        beta_ready = sem("beta_ready")
        hhi_ready = sem("hhi_ready")
        hlo_ready = sem("hlo_ready")
        l1_done = sem("l1_done")
        r_ready = sem("r_ready")
        rhi_ready = sem("rhi_ready")
        rlo_ready = [sem("rlo_ready0"), sem("rlo_ready1")]
        src3_ready = sem("src3_ready")
        v2_done = sem("v2_done")
        tab_ready = sem("tab_ready")
        l2_done = sem("l2_done")
        out_ready = sem("out_ready")
        dve_stats = sem("dve_stats")
        dve_rstd = sem("dve_rstd")
        dve_top = sem("dve_top")
        dve_pre = sem("dve_pre")
        dve_acc = sem("dve_acc")
        dve_prod = sem("dve_prod")
        dve_vhi = sem("dve_vhi")
        dve_rest = sem("dve_rest")
        dve_mid = sem("dve_mid")
        dve_deg = sem("dve_deg")
        dve_group = sem("dve_group")
        pool_group = sem("pool_group")
        dve_init = sem("dve_init")

        block = ctx.enter_context(nc.Block())

        def slots(eng, slot):
            if LOOPS > 1:
                with eng.Fori(0, LOOPS, 1) as it:
                    for j in range(RING):
                        slot(it, j, False)
            else:
                for it in range(LOOPS):
                    for j in range(RING):
                        slot(it, j, False)
            for j in range(RING):
                slot(LOOPS, j, True)

        def at(it, j, per, k):
            return it * (RING * per) + (per * j + k)

        def at_group(it, j, per, k):
            return it * (RING // G * per) + (per * (j // G) + k)

        @block.sync
        def _(sp):
            sp.dma_start(xb[:, 0], x[0].rearrange("(k p) n -> p k n", p=P)).then_inc(x_loaded[0], 16)
            sp.dma_start(cst[:], small).then_inc(consts_loaded, 16)
            sp.dma_start(r[:].rearrange("p k n -> p (k n)")[:, 0:T_WID], staged).then_inc(consts_loaded, 16)
            sp.dma_start(w[:], w_t.rearrange("(k p) n -> p k n", p=P)).then_inc(consts_loaded, 16)
            sp.dma_start(bias1[:], b1).then_inc(consts_loaded, 16)
            sp.dma_start(bias2[:], b2).then_inc(consts_loaded, 16)
            for b in range(1, RING):
                sp.dma_start(xb[:, b], x[b].rearrange("(k p) n -> p k n", p=P)).then_inc(x_loaded[b], 16)

            x_all = x.rearrange("b (k p) n -> p b k n", p=P)
            out_all = out.rearrange("b (k p) n -> p b k n", p=P)

            def slot(it, j, last):
                b = it * RING + j
                sp.wait_ge(out_ready, at(it, j, 4, 8))
                src = xb[:, j:j + 1]
                dst = out_all[:, b:b + 1] if isinstance(b, int) else out_all[:, bass.ds(b, 1)]
                sp.dma_start(dst, src).then_inc(x_stored[j], 16)
                if not last:
                    sp.wait_ge(x_stored[j], it * 16 + 16)
                    nb = it * RING + (j + RING)
                    nxt = x_all[:, nb:nb + 1] if isinstance(nb, int) else x_all[:, bass.ds(nb, 1)]
                    sp.dma_start(xb[:, j:j + 1], nxt).then_inc(x_loaded[j], 16)

            slots(sp, slot)
            for j in range(RING):
                sp.wait_ge(x_stored[j], 16 * (NB // RING))

        @block.scalar
        def _(act):
            def root(it, j, k):
                act.wait_ge(stats_ready, at(it, j, 1, k + 1))
                nc.scalar.activation(std[:], mv[:, :, 1], ACT.Sqrt,
                                     bias=c_("eps")).then_inc(std_ready, 1)

            def normalise(it, j, k, kf):
                a = (j + k) % RING
                if kf == 0:
                    act.wait_ge(norm_ready, at(it, j, 1, k + 1))
                last = nc.scalar.activation(
                    hb[:, a, kf], xb[:, a, kf], ACT.Relu, bias=nmean[:, a % 2, kf:kf + 1],
                    scale=rstd[:, a % 2, kf:kf + 1], accum_out=h_tot[:, a, kf:kf + 1])
                if kf == KF - 1:
                    last.then_inc(h_ready, 1)

            def split_sum(it, j, k):
                act.wait_ge(hsum_ready, at(it, j, 1, k + 1))
                if not (isinstance(it, int) and it == 0 and j + k == 0):
                    act.wait_ge(fv_done, at(it, j, 1, k))
                nc.scalar.activation(hsum_hi[:], hsum[:], ACT.Copy).then_inc(hshi_ready, 1)

            def take_sums(it, j, k):
                act.wait_ge(fv_done, at(it, j, 1, k + G))
                nc.scalar.activation(fv[:, 0:N], ps_fv[0:G], ACT.Copy).then_inc(fv_copied, 1)

            def split_h(it, j, k, half):
                a = (j + k) % RING
                n = slice(half * H, half * H + H)
                nc.scalar.activation(h_hi[:, :, n], hb[:, a, :, n], ACT.Copy).then_inc(hhi_ready, 1)

            def relu(it, j, half, m):
                u = 2 * half + m
                par = j % 2
                act.wait_ge(l1_done, at(it, j, 4, u + 1))
                if u == 0:
                    act.wait_ge(beta_ready, at(it, j, 1, 1))
                com = dict(bias=beta[:, par, m, 0:1], scale=1.0 / (D0 * D0))
                if half == 0:
                    nc.scalar.activation(r[:, m, K_TOP + 1:H], ps[u][:, K_TOP + 1:H], ACT.Relu,
                                         accum_out=acc[:, m, 0:1], **com)
                    nc.scalar.activation(r[:, m, 0:1], ps[u][:, 0:1], ACT.Relu,
                                         accum_out=acc[:, m, 1:2], **com)
                    last = nc.scalar.activation(
                        r[:, m, 1:K_TOP + 1], ps[u][:, 1:K_TOP + 1], ACT.Relu, bias=beta[:, par, m, 1:2],
                        scale=rdeg2[:, (j // G) % 2, j % G:j % G + 1],
                        accum_out=src2[:, par, m, C_STATIC:C_STATIC + 1])
                else:
                    last = nc.scalar.activation(r[:, m, H:N], ps[u][:], ACT.Relu,
                                                accum_out=acc[:, m, 2:3], **com)
                last.then_inc(r_ready, 1)

            def split_r(it, j, half, more):
                act.wait_ge(r_ready, at(it, j, 4, 2 * half + 2))
                if half == 1 and more:
                    act.wait_ge(sums_ready, at(it, j, 1, 2))
                n = slice(half * H, half * H + H)
                nc.scalar.activation(r_hi[:, :, n], r[:, :, n], ACT.Copy).then_inc(rhi_ready, 1)

            act.wait_ge(consts_ready, 1)
            for a in range(LEAD):
                root(0, 0, a)
                normalise(0, 0, a, 0)
                normalise(0, 0, a, 1)
                if a == 0:
                    act.wait_ge(h_ready, 1)
                    split_h(0, 0, 0, 0)
                    split_h(0, 0, 0, 1)
                split_sum(0, 0, a)
                if a == G - 1:
                    take_sums(0, 0, 0)

            def slot(it, j, last):
                more = not (last and j == RING - 1)
                ahead = not (last and j >= RING - LEAD)
                relu(it, j, 0, 0)
                relu(it, j, 0, 1)
                if ahead:
                    root(it, j, LEAD)
                split_r(it, j, 0, more)
                if j % G == 2 and not (last and j >= G):
                    take_sums(it, j, 2)
                if ahead:
                    normalise(it, j, LEAD, 0)
                relu(it, j, 1, 0)
                relu(it, j, 1, 1)
                split_r(it, j, 1, more)
                if ahead:
                    normalise(it, j, LEAD, 1)
                if more:
                    split_h(it, j, 1, 0)
                if ahead:
                    split_sum(it, j, LEAD)
                if more:
                    split_h(it, j, 1, 1)

            slots(act, slot)

        @block.gpsimd
        def _(pool):
            def sum_chunks(it, j, k):
                a = (j + k) % RING
                pool.wait_ge(h_ready, at(it, j, 1, k + 1))
                if not (isinstance(it, int) and it == 0 and j + k == 0):
                    pool.wait_ge(hslo_ready, at(it, j, 1, k))
                nc.gpsimd.tensor_tensor(hsum[:], hb[:, a, 0], hb[:, a, 1], ALU.add).then_inc(hsum_ready, 1)

            def split_sum(it, j, k):
                pool.wait_ge(hshi_ready, at(it, j, 1, k + 1))
                nc.gpsimd.tensor_tensor(hsum_lo[:], hsum[:], hsum_hi[:].bitcast(F32),
                                        ALU.subtract).then_inc(hslo_ready, 1)

            def split_r(it, j, half):
                n = slice(half * H, half * H + H)
                pool.wait_ge(rhi_ready, at(it, j, 2, half + 1))
                nc.gpsimd.tensor_tensor(r_lo[:, :, n], r[:, :, n], r_hi[:, :, n].bitcast(F32),
                                        ALU.subtract).then_inc(rlo_ready[half], 1)

            def split_h(it, j, k, half):
                a = (j + k) % RING
                n = slice(half * H, half * H + H)
                pool.wait_ge(hhi_ready, at(it, j, 2, 2 * k + half + 1))
                nc.gpsimd.tensor_tensor(h_lo[:, :, n], hb[:, a, :, n], h_hi[:, :, n].bitcast(F32),
                                        ALU.subtract).then_inc(hlo_ready, 1)

            def sources(it, j, k):
                t = j + k
                a, par, gp, g = t % RING, t % 2, (t // G) % 2, t % G
                rd = rdeg[:, gp, g]
                pool.wait_ge(sums_ready, at(it, j, 1, k + 1))
                if t % G == 0:
                    pool.wait_ge(deg_ready, at_group(it, t, 1, 1))
                for c, sums in ((slice(0, 4), h_tot[:, a]), (slice(4, 8, 2), h_top[:, par]),
                                (slice(5, 8, 2), h_sta[:, par])):
                    n = len(range(*c.indices(NCLS)))
                    last = nc.gpsimd.tensor_tensor(
                        src1[:, :, c], rd[:, c].unsqueeze(1).broadcast_to([P, KF, n]),
                        sums.unsqueeze(2).broadcast_to([P, KF, n]), ALU.mult)
                last.then_inc(src1_ready, 1)

            def tables(it, j, k):
                t = j + k
                gp = (t // G) % 2
                mx = mix[:, gp]
                shape = [P, G, NCLS, NCLS]
                pool.wait_ge(deg_ready, at_group(it, t, 1, 1))
                nc.gpsimd.tensor_tensor(
                    mx[:, :, :, C_STATIC], c_("adj_static").unsqueeze(1).broadcast_to([P, G, NCLS]),
                    deg[:, :, C_STATIC].unsqueeze(2).broadcast_to([P, G, NCLS]),
                    ALU.mult).then_inc(pool_group, 1)
                nc.gpsimd.tensor_copy(mx[:, :, :, C_COMMON],
                                      c_("adj_common").unsqueeze(1).broadcast_to([P, G, NCLS])).then_inc(pool_group, 1)
                pool.wait_ge(pool_group, at_group(it, t, 3, 2))
                nc.gpsimd.tensor_tensor(
                    mx, mx, c_("keep_own").rearrange("p (c s) -> p c s", c=NCLS).unsqueeze(1).broadcast_to(shape),
                    ALU.add).then_inc(pool_group, 1)
                pool.wait_ge(pool_group, at_group(it, t, 3, 3))
                nc.gpsimd.tensor_tensor(
                    mx, mx, rdeg[:, gp].unsqueeze(3).broadcast_to(shape), ALU.mult).then_inc(mix_ready, 1)

            pool.wait_ge(consts_ready, 1)
            for a in range(LEAD):
                sum_chunks(0, 0, a)
                if a == 0:
                    split_h(0, 0, 0, 0)
                    split_h(0, 0, 0, 1)
                split_sum(0, 0, a)
            tables(0, 0, 0)
            sources(0, 0, 0)

            def slot(it, j, last):
                more = not (last and j == RING - 1)
                ahead = not (last and j >= RING - LEAD)
                split_r(it, j, 0)
                if more:
                    sources(it, j, 1)
                if ahead:
                    sum_chunks(it, j, LEAD)
                if more:
                    split_h(it, j, 1, 0)
                if ahead:
                    split_sum(it, j, LEAD)
                if more:
                    split_h(it, j, 1, 1)
                if j % G == G - 1 and not (last and j >= G):
                    tables(it, j, 1)

            slots(pool, slot)

        @block.tensor
        def _(pe):
            def column_sums(it, j, k):
                t = j + k
                pe.wait_ge(hslo_ready, at(it, j, 1, k + 1))
                if t % G == 0 and not (isinstance(it, int) and it == 0 and t == 0):
                    pe.wait_ge(fv_copied, at_group(it, t, 1, 0))
                row = col[:, G - 1 - t % G:G - 1 - t % G + P]
                for half in range(2):
                    n = slice(half * H, half * H + H)
                    for part in (hsum_hi, hsum_lo):
                        last = nc.tensor.matmul(
                            ps_fv[:, n], row, part[:, n], start=(t % G == 0 and part is hsum_hi),
                            stop=(t % G == G - 1 and part is hsum_lo), skip_group_check=True)
                last.then_inc(fv_done, 1)

            def spread_group(it, j, k):
                t = j + k
                pe.wait_ge(code_ready, at_group(it, t, 1, 1))
                for half in range(2):
                    n = slice(half * H, half * H + H)
                    last = nc.tensor.matmul(ps_c[:, n], spread[:, G], code[:, n], start=True, stop=True)
                last.then_inc(spread_done, 1)

            def spread_counts(it, j, k):
                t = j + k
                pe.wait_ge(cntd_ready, at_group(it, t, 1, 1))
                nc.tensor.matmul(NBC, c_("ones"), cnt_d[:], start=True, stop=True).then_inc(cnt_done, 1)

            def spread_batch(it, j, k):
                t = j + k
                if t % G == 0:
                    pe.wait_ge(cnt_copied, at_group(it, t, 1, 1))
                for half in range(2):
                    n = slice(half * H, half * H + H)
                    last = nc.tensor.matmul(ps_c[:, n], spread[:, t % G], code[:, n], start=True, stop=True)
                last.then_inc(cls_done, 1)

            def class_values(it, j, k):
                pe.wait_ge(src1_ready, at(it, j, 1, k + 1))
                pe.wait_ge(sums_ready, at(it, j, 1, k + 1))
                for m in range(KF):
                    for kf in range(KF):
                        last = nc.tensor.matmul(X1[:, m], w[:, kf, m * P:m * P + P], src1[:, kf],
                                                start=(kf == 0), stop=(kf == KF - 1))
                last.then_inc(x1_done, 1)

            def product(half, hi, lo, lo_ready):
                n = slice(half * H, half * H + H)
                for part in range(2):
                    if part:
                        pe.wait_ge(*lo_ready)
                    for m in range(KF):
                        mm = slice(m * P, m * P + P)
                        for kf in range(KF):
                            for wt, mov in (((w_hi, lo),) if part else ((w_hi, hi), (w_lo, hi))):
                                nc.tensor.matmul(ps[2 * half + m][:], wt[:, kf, mm], mov[:, kf, n],
                                                 start=(part == 0 and kf == 0 and wt is w_hi), stop=False,
                                                 skip_group_check=True)

            def layer1(it, j, half):
                n = slice(half * H, half * H + H)
                pe.wait_ge(hhi_ready, at(it, j, 2, half + 1))
                pe.wait_ge(out_ready, at(it, j, 4, 2 * half + 2))
                product(half, h_hi, h_lo, (hlo_ready, at(it, j, 2, half + 1)))
                for m in range(KF):
                    nc.tensor.matmul(ps[2 * half + m][:], mask[:, j % G], onehot[:, (j // G) % 2, n],
                                     start=False, stop=True, skip_group_check=True).then_inc(l1_done, 1)

            def layer2(it, j, half):
                pe.wait_ge(rhi_ready, at(it, j, 2, half + 1))
                product(half, r_hi, r_lo, (rlo_ready[half], at(it, j, 1, 1)))

            def class_terms(it, j):
                pe.wait_ge(src3_ready, at(it, j, 1, 1))
                a = 96 - 32 * (j % G)
                for kf in range(KF):
                    last = nc.tensor.matmul(V2, src3[:, kf, a:a + P], w[:, kf],
                                            start=(kf == 0), stop=(kf == KF - 1))
                last.then_inc(v2_done, 1)

            def add_terms(it, j):
                pe.wait_ge(tab_ready, at(it, j, 1, 1))
                for u in range(4):
                    half, m = divmod(u, 2)
                    n = slice(half * H, half * H + H)
                    nc.tensor.matmul(ps[u][:], tab[:, m * P:m * P + P], onehot[:, (j // G) % 2, n],
                                     start=False, stop=True, skip_group_check=True).then_inc(l2_done, 1)

            pe.wait_ge(consts_ready, 1)
            for a in range(G):
                column_sums(0, 0, a)
            spread_group(0, 0, 0)
            column_sums(0, 0, G)
            spread_counts(0, 0, 0)
            spread_batch(0, 0, 0)
            class_values(0, 0, 0)

            def slot(it, j, last):
                more = not (last and j == RING - 1)
                grouped = j % G == G - 1 and not (last and j >= G)
                layer1(it, j, 0)
                if not (last and j >= RING - LEAD + 1):
                    column_sums(it, j, LEAD - 1)
                if more:
                    pe.wait_ge(beta_ready, at(it, j, 1, 1))
                    if grouped:
                        spread_group(it, j, 1)
                    else:
                        spread_batch(it, j, 1)
                layer1(it, j, 1)
                if grouped:
                    spread_counts(it, j, 1)
                    spread_batch(it, j, 1)
                layer2(it, j, 0)
                if more:
                    class_values(it, j, 1)
                class_terms(it, j)
                layer2(it, j, 1)
                add_terms(it, j)

            slots(pe, slot)

        @block.vector
        def _(dve):
            def hold(s, value):
                dve.wait_ge(s, value)
                nc.vector.memset(cell[:], 0.0)

            def moments(it, j, k):
                a = (j + k) % RING
                q = (j + k) // RING
                dve.wait_ge(x_loaded[a], it * 16 + 16 * (q + 1))
                for kf in range(KF):
                    for half in range(2):
                        last = nc.vector.bn_stats(stats[:, kf, half], xb[:, a, kf, half * H:half * H + H])
                last.then_inc(dve_stats, 1)
                hold(dve_stats, at(it, j, 1, k + 1))
                for kf in range(KF):
                    last = nc.vector.bn_aggr(mv[:, kf], stats[:, kf].rearrange("p a b -> p (a b)"))
                last.then_inc(stats_ready, 1)

            def scales(it, j, k):
                a = (j + k) % RING
                dve.wait_ge(std_ready, at(it, j, 1, k + 1))
                nc.vector.reciprocal(rstd[:, a % 2], std[:]).then_inc(dve_rstd, 1)
                dve.wait_ge(dve_rstd, at(it, j, 1, k + 1))
                nc.vector.scalar_tensor_tensor(nmean[:, a % 2], mv[:, :, 0], -1.0, rstd[:, a % 2],
                                               ALU.mult, ALU.mult).then_inc(norm_ready, 1)

            def node_sums(it, j, k):
                t = j + k
                a, par = t % RING, t % 2
                dve.wait_ge(h_ready, at(it, j, 1, k + 1))
                nc.vector.tensor_reduce(h_sta[:, par], hb[:, a, :, 1:K_TOP + 1], AX_X, ALU.add)
                dve.wait_ge(cls_done, at(it, j, 1, k + 1))
                for kf in range(KF):
                    if kf > 0:
                        dve.wait_ge(dve_top, at(it, j, 1, k + 1))
                    last = nc.vector.scalar_tensor_tensor(
                        junk, ps_c[:].rearrange("p (h n) -> p h n", h=2), 4.0,
                        hb[:, a, kf].rearrange("p (h n) -> p h n", h=2), ALU.is_lt, ALU.mult,
                        accum_out=h_top[:, par, kf:kf + 1])
                    last.then_inc(dve_top if kf == 0 else sums_ready, 1)

            def class_biases(it, j, k):
                t = j + k
                par, gp, g = t % 2, (t // G) % 2, t % G
                dve.wait_ge(x1_done, at(it, j, 1, k + 1))
                nc.vector.tensor_tensor(pre[:], X1, bias1[:].unsqueeze(2).broadcast_to([P, KF, NCLS]),
                                        ALU.add).then_inc(dve_pre, 1)
                dve.wait_ge(dve_pre, at(it, j, 1, k + 1))
                nc.vector.tensor_scalar(src2[:, par], pre[:], 0.0, None, ALU.max)
                nc.vector.tensor_tensor(
                    beta[:, par], pre[:, :, C_COMMON:NCLS:2],
                    rdeg[:, gp, g, C_COMMON:NCLS:2].unsqueeze(1).broadcast_to([P, KF, 2]),
                    ALU.mult).then_inc(beta_ready, 1)

            def split_r(it, j, half):
                n = slice(half * H, half * H + H)
                dve.wait_ge(rhi_ready, at(it, j, 2, half + 1))
                nc.vector.tensor_tensor(r_lo[:, :, n], r[:, :, n], r_hi[:, :, n].bitcast(F32),
                                        ALU.subtract).then_inc(rlo_ready[half], 1)

            def class_terms(it, j):
                par, gp, g = j % 2, (j // G) % 2, j % G
                dve.wait_ge(r_ready, at(it, j, 4, 4))
                nc.vector.tensor_reduce(src2[:, par, :, C_COMMON], acc[:], AX_X, ALU.add).then_inc(dve_acc, 1)
                if g == 0:
                    dve.wait_ge(mix_ready, at_group(it, j, 1, 1))
                dve.wait_ge(dve_acc, at(it, j, 1, 1))
                for kf in range(KF):
                    last = nc.vector.tensor_tensor(
                        prod[:, kf], src2[:, par, kf].unsqueeze(1).broadcast_to([P, NCLS, NCLS]),
                        mix[:, gp, g], ALU.mult)
                last.then_inc(dve_prod, 1)
                dve.wait_ge(dve_prod, at(it, j, 1, 1))
                for dup in range(3):
                    last = nc.vector.tensor_reduce(src3[:, :, 96 + 8 * dup:104 + 8 * dup], prod[:], AX_X, ALU.add)
                last.then_inc(src3_ready, 1)

            def table(it, j):
                dve.wait_ge(v2_done, at(it, j, 1, 1))
                nc.vector.tensor_copy(v_hi[:], V2).then_inc(dve_vhi, 1)
                dve.wait_ge(dve_vhi, at(it, j, 1, 1))
                nc.vector.scalar_tensor_tensor(v_rest[:], v_hi[:], c_("less_hi"), V2,
                                               ALU.mult, ALU.add).then_inc(dve_rest, 1)
                dve.wait_ge(dve_rest, at(it, j, 1, 1))
                nc.vector.tensor_copy(v_hi[:], v_rest[:]).then_inc(dve_mid, 1)
                dve.wait_ge(dve_mid, at(it, j, 1, 1))
                nc.vector.scalar_tensor_tensor(tab[:], v_hi[:], c_("less_mid"), v_rest[:],
                                               ALU.mult, ALU.add).then_inc(tab_ready, 1)

            def finish(it, j):
                for u in range(4):
                    half, m = divmod(u, 2)
                    n = slice(half * H, half * H + H)
                    dve.wait_ge(l2_done, at(it, j, 4, u + 1))
                    nc.vector.scalar_tensor_tensor(xb[:, j, m, n], ps[u][:], bias2[:, m:m + 1],
                                                   xb[:, j, m, n], ALU.add, ALU.add).then_inc(out_ready, 1)

            def top_nodes(it, j, k, part):
                t = j + k

                def link(ins, n):
                    ins.then_inc(dve_group, 1)
                    hold(dve_group, at_group(it, t, 5, n))

                if part == 0:
                    if not (isinstance(it, int) and it == 0 and t == 0):
                        dve.wait_ge(cls_done, at(it, j, 1, k))
                    nc.vector.memset(first[:], PAST)
                    nc.vector.memset(fv[:, N:], PAST)
                    hold(fv_copied, at_group(it, t, 1, 1))
                    link(nc.vector.max(best[:], fv[:, 0:N]), 1)
                    nc.vector.tensor_scalar(code[0:G], fv[:, 0:N], 0.0, 4.0, ALU.is_equal,
                                            ALU.add).then_inc(zero_ready, 1)
                    link(nc.vector.tensor_copy(first[:, 0:1], best[:, 0:1]), 2)
                    link(nc.vector.match_replace(fv[:], first[:], fv[:], T_MARK), 3)
                    dve.wait_ge(zero_ready, at_group(it, t, 1, 1))
                    nc.vector.tensor_scalar(code[0:G, 1:K_TOP + 1], code[0:G, 1:K_TOP + 1], 2.0, None,
                                            ALU.add)
                elif part == 1:
                    link(nc.vector.max(best[:], fv[:, 0:N]), 4)
                    nc.vector.match_replace(fv[:, 0:N], best[:], fv[:, 0:N], M_MARK).then_inc(dve_group, 1)
                else:
                    dve.wait_ge(dve_group, at_group(it, t, 5, 5))
                    nc.vector.scalar_tensor_tensor(code[0:G], fv[:, 0:N], 0.0, code[0:G], ALU.min,
                                                   ALU.add).then_inc(code_ready, 1)

            def group_onehot(it, j, k):
                t = j + k
                gp = (t // G) % 2
                dve.wait_ge(spread_done, at_group(it, t, 1, 1))
                nc.vector.tensor_scalar(onehot[:, gp], ps_c[:], c_("cls"), None, ALU.is_equal, ALU.add,
                                        accum_out=cnt[:]).then_inc(onehot_ready, 1)
                dve.wait_ge(onehot_ready, at_group(it, t, 1, 1))
                nc.vector.tensor_scalar(cnt_d[:], c_("pick_n"), cnt[:], None, ALU.mult).then_inc(cntd_ready, 1)

            def group_degrees(it, j, k):
                t = j + k
                gp = (t // G) % 2
                shape = [P, G, NCLS, NCLS]
                dve.wait_ge(cnt_done, at_group(it, t, 1, 1))
                nc.vector.tensor_copy(cnt_b[:].rearrange("p g c -> p (g c)"), NBC).then_inc(cnt_copied, 1)
                dve.wait_ge(cnt_copied, at_group(it, t, 1, 1))
                nc.vector.tensor_tensor(
                    mix[:, gp], c_("adj").rearrange("p (c s) -> p c s", c=NCLS).unsqueeze(1).broadcast_to(shape),
                    cnt_b[:].unsqueeze(2).broadcast_to(shape), ALU.mult).then_inc(dve_deg, 1)
                dve.wait_ge(dve_deg, at_group(it, t, 3, 1))
                nc.vector.tensor_reduce(deg[:], mix[:, gp], AX_X, ALU.add).then_inc(dve_deg, 1)
                dve.wait_ge(dve_deg, at_group(it, t, 3, 2))
                nc.vector.tensor_tensor(deg[:], deg[:], c_("own").unsqueeze(1).broadcast_to([P, G, NCLS]),
                                        ALU.add).then_inc(dve_deg, 1)
                dve.wait_ge(dve_deg, at_group(it, t, 3, 3))
                nc.vector.reciprocal(rdeg[:, gp], deg[:]).then_inc(deg_ready, 1)
                dve.wait_ge(deg_ready, at_group(it, t, 1, 1))
                nc.vector.tensor_tensor(rdeg2[:, gp], rdeg[:, gp, :, C_STATIC], rdeg[:, gp, :, C_STATIC],
                                        ALU.mult)

            nc.vector.memset(code[:], 0.0).then_inc(zeroed, 1)
            nc.vector.memset(src3[:], 0.0).then_inc(zeroed, 1)
            dve.wait_ge(consts_loaded, 16 * 5)
            flat = r[:].rearrange("p k n -> p (k n)")
            nc.vector.tensor_copy(mask[:].rearrange("p g n -> p (g n)"), flat[:, 0:G * P])
            nc.vector.tensor_copy(spread[:].rearrange("p g n -> p (g n)"), flat[:, G * P:(2 * G + 1) * P])
            nc.vector.tensor_copy(col[:], flat[:, (2 * G + 1) * P:T_WID])
            nc.vector.tensor_copy(w_hi[:], w[:]).then_inc(dve_init, 1)
            dve.wait_ge(dve_init, 1)
            nc.vector.tensor_tensor(w_lo[:], w[:], w_hi[:].bitcast(F32), ALU.subtract).then_inc(out_ready, 4)
            dve.wait_ge(out_ready, 4)
            nc.vector.memset(cell[:], 0.0).then_inc(consts_ready, 1)

            for a in range(G):
                moments(0, 0, a)
                scales(0, 0, a)
            moments(0, 0, G)
            scales(0, 0, G)
            top_nodes(0, 0, 0, 0)
            top_nodes(0, 0, 0, 1)
            top_nodes(0, 0, 0, 2)
            group_onehot(0, 0, 0)
            moments(0, 0, G + 1)
            scales(0, 0, G + 1)
            group_degrees(0, 0, 0)
            node_sums(0, 0, 0)
            class_biases(0, 0, 0)

            def slot(it, j, last):
                more = not (last and j == RING - 1)
                ahead = not (last and j >= RING - LEAD)
                if ahead:
                    moments(it, j, LEAD)
                    scales(it, j, LEAD)
                if j % G == G - 1 and not (last and j >= G):
                    group_onehot(it, j, 1)
                    group_degrees(it, j, 1)
                if more:
                    node_sums(it, j, 1)
                if j % G == 2 and not (last and j >= G):
                    top_nodes(it, j, 2, 0)
                class_terms(it, j)
                split_r(it, j, 1)
                if more:
                    class_biases(it, j, 1)
                table(it, j)
                if j % G == 2 and not (last and j >= G):
                    top_nodes(it, j, 2, 1)
                finish(it, j)
                if j % G == 2 and not (last and j >= G):
                    top_nodes(it, j, 2, 2)

            slots(dve, slot)


def kernel(x, adj, L0_gnn_b1, L0_gnn_b2):
    import concourse.bacc as bacc
    from concourse.bass_utils import run_bass_kernel_spmd

    small, staged = constants()
    arrays = {
        "x": np.ascontiguousarray(x),
        "w_t": np.ascontiguousarray(np.asarray(adj).T),
        "b1": np.ascontiguousarray(np.asarray(L0_gnn_b1).reshape(KF, P).T),
        "b2": np.ascontiguousarray(np.asarray(L0_gnn_b2).reshape(KF, P).T),
        "small": small,
        "staged": staged,
    }
    nc = bacc.Bacc("TRN2", target_bir_lowering=False, num_devices=1)
    ins = [nc.dram_tensor(name, a.shape, F32, kind="ExternalInput").ap() for name, a in arrays.items()]
    out = nc.dram_tensor("out", arrays["x"].shape, F32, kind="ExternalOutput").ap()
    build(nc, *ins, out)
    result = run_bass_kernel_spmd(nc, [arrays], core_ids=[0])
    return result.results[0]["out"]
```

```python
from contextlib import ExitStack

import numpy as np

import concourse.bass as bass
from concourse import mybir

F32 = mybir.dt.float32
F32R = mybir.dt.float32r
BF16 = mybir.dt.bfloat16
ALU = mybir.AluOpType
ACT = mybir.ActivationFunctionType
AX_X = mybir.AxisListType.X

P = 128
KF = 2
N = 1024
H = 512
G = 4
RING = 8
LEAD = 6
LATE = (2, 3)
K_TOP = 8
NCLS = 8
T_MARK = -1e-30
M_MARK = -4.0
PAST = -5.0
BIG = -(2.0 ** 120)
C_COMMON, C_STATIC = 4, 6
D0 = float(K_TOP + 1)



def class_tables():
    bits = [(c & 1, 1 - (c >> 2), (c >> 1) & 1) for c in range(NCLS)]
    pick = np.array([[(1 - zc) * ms + zc * es for _, ms, es in bits] for zc, _, _ in bits], np.float32)
    adj = np.maximum(pick, pick.T)
    own = 1.0 - np.diag(adj)
    return adj, own


COLS = {}


def constants():
    adj, own = class_tables()
    keep_own = np.diag(np.where(np.isin(np.arange(NCLS), (C_COMMON, C_STATIC)), 0.0, own))
    row = np.arange(P) % 32
    parts = [
        ("cls", np.where(row < 24, row % 8, -1.0)[:, None]),
        ("less_hi", np.where((row >= 8) & (row < 24), -1.0, 0.0)[:, None]),
        ("less_mid", np.where((row >= 16) & (row < 24), -1.0, 0.0)[:, None]),
        ("eps", np.full((P, 1), 1e-5)),
        ("adj", np.tile(adj.reshape(1, -1), (P, 1))),
        ("keep_own", np.tile(keep_own.reshape(1, -1), (P, 1))),
        ("own", np.tile(own[None], (P, 1))),
        ("adj_common", np.tile(adj[None, :, C_COMMON] * D0, (P, 1))),
        ("adj_static", np.tile(adj[None, :, C_STATIC], (P, 1))),
        ("pick_n", np.array([[float(p % 32 < NCLS and (p // 32) * NCLS + p % 32 == q) for q in range(G * NCLS)]
                             for p in range(P)])),
        ("ones", np.ones((P, P))),
    ]
    at = 0
    for name, a in parts:
        COLS[name] = (at, at + a.shape[1])
        at += a.shape[1]
    small = np.concatenate([a for _, a in parts], 1).astype(np.float32)
    mask = np.zeros((P, G, P), np.float32)
    spread = np.zeros((P, G + 1, P), np.float32)
    for j in range(G):
        for c in range(NCLS):
            if c not in (C_COMMON, C_STATIC):
                mask[32 * j + c, j] = BIG
        spread[j, j] = 1.0
        spread[j, G, 32 * j:32 * j + 32] = 1.0
    col = np.tile((np.arange(P + G - 1) == G - 1)[None], (P, 1)).astype(np.float32)
    staged = np.concatenate([mask.reshape(P, -1), spread.reshape(P, -1), col], 1)
    return small, staged


def build(nc, x, w_t, b1, b2, small, staged, out):
    NB = x.shape[0]
    LOOPS = NB // RING - 1
    S_WID, T_WID = small.shape[1], staged.shape[1]

    with ExitStack() as ctx:
        def sb(name, shape, dt=F32):
            return ctx.enter_context(nc.sbuf_tensor(name, shape, dt))

        def pb(name, shape, dt=F32):
            return ctx.enter_context(nc.psum_tensor(name, shape, dt))

        def sem(name):
            return ctx.enter_context(nc.semaphore(name))

        xb = sb("xb", [P, RING, KF, N])
        hb = sb("hb", [P, RING, KF, N])
        h_hi = sb("h_hi", [P, KF, N], F32R)
        h_lo = sb("h_lo", [P, KF, N], F32R)
        r = sb("r", [P, KF, N])
        r_hi = sb("r_hi", [P, KF, N], F32R)
        r_lo = sb("r_lo", [P, KF, N], F32R)
        hsum = sb("hsum", [P, N])
        hsum_hi = sb("hsum_hi", [P, N], F32R)
        hsum_lo = sb("hsum_lo", [P, N], F32R)
        col = sb("col", [P, P + G - 1], F32R)
        fv = sb("fv", [G, N + 8])
        code = sb("code", [P, N], BF16)
        onehot = sb("onehot", [P, 2, N], BF16)
        cell = sb("cell", [1, 1])
        w = sb("w", [P, KF, KF * P])
        w_hi = sb("w_hi", [P, KF, KF * P], F32R)
        w_lo = sb("w_lo", [P, KF, KF * P], F32R)
        cst = sb("cst", [P, S_WID])
        mask = sb("mask", [P, G, P], BF16)
        spread = sb("spread", [P, G + 1, P], BF16)
        bias1 = sb("bias1", [P, KF])
        bias2 = sb("bias2", [P, KF])
        stats = sb("stats", [P, KF, 2, 6])
        mv = sb("mv", [P, KF, 2])
        std = sb("std", [P, KF])
        rstd = sb("rstd", [P, 2, KF])
        nmean = sb("nmean", [P, 2, KF])
        h_tot = sb("h_tot", [P, RING, KF])
        h_top = sb("h_top", [P, 2, KF])
        h_sta = sb("h_sta", [P, 2, KF])
        best = sb("best", [G, 8])
        first = sb("first", [G, 8])
        cnt = sb("cnt", [P, 1])
        cnt_d = sb("cnt_d", [P, G * NCLS])
        cnt_b = sb("cnt_b", [P, G, NCLS])
        mix = sb("mix", [P, 2, G, NCLS, NCLS])
        deg = sb("deg", [P, G, NCLS])
        rdeg = sb("rdeg", [P, 2, G, NCLS])
        rdeg2 = sb("rdeg2", [P, 2, G])
        src1 = sb("src1", [P, KF, NCLS])
        pre = sb("pre", [P, KF, NCLS])
        src2 = sb("src2", [P, 2, KF, NCLS])
        beta = sb("beta", [P, 2, KF, 2])
        acc = sb("acc", [P, KF, 3])
        prod = sb("prod", [P, KF, NCLS, NCLS])
        src3 = sb("src3", [P, KF, 96 + P])
        v_hi = sb("v_hi", [P, KF * P], BF16)
        v_rest = sb("v_rest", [P, KF * P])
        tab = sb("tab", [P, KF * P], BF16)

        ps = [pb(f"ps{u}", [P, H]) for u in range(4)]
        ps_fv = pb("ps_fv", [P, N])
        ps_c = pb("ps_c", [P, N])
        V2 = ps_c[:, H:H + KF * P]
        X1 = ps_c[:, 0:KF * NCLS].rearrange("p (m c) -> p m c", m=KF)
        NBC = ps_c[:, H - G * NCLS:H]

        junk = r_hi[:, :, H:N]

        def in_first(it, t):
            return isinstance(it, int) and it == 0 and t < G

        def sum_buffers(it, t):
            if in_first(it, t):
                return r[:, t % 2], r_hi[:, t % 2], r_lo[:, t % 2]
            return hsum[:], hsum_hi[:], hsum_lo[:]

        def c_(name):
            a, b = COLS[name]
            return cst[:, a:b]

        x_loaded = [sem(f"x_loaded{i}") for i in range(RING)]
        x_stored = [sem(f"x_stored{i}") for i in range(RING)]
        small_loaded = sem("small_loaded")
        consts_loaded = sem("consts_loaded")
        zeroed = sem("zeroed")
        consts_ready = sem("consts_ready")
        stats_ready = sem("stats_ready")
        std_ready = sem("std_ready")
        norm_ready = sem("norm_ready")
        h_ready = sem("h_ready")
        hsum_ready = sem("hsum_ready")
        hshi_ready = sem("hshi_ready")
        hslo_ready = sem("hslo_ready")
        fv_done = sem("fv_done")
        fv_copied = sem("fv_copied")
        zero_ready = sem("zero_ready")
        code_ready = sem("code_ready")
        spread_done = sem("spread_done")
        onehot_ready = sem("onehot_ready")
        cntd_ready = sem("cntd_ready")
        cnt_done = sem("cnt_done")
        cnt_copied = sem("cnt_copied")
        deg_ready = sem("deg_ready")
        mix_ready = sem("mix_ready")
        cls_done = sem("cls_done")
        sums_ready = sem("sums_ready")
        src1_ready = sem("src1_ready")
        x1_done = sem("x1_done")
        beta_ready = sem("beta_ready")
        hhi_ready = sem("hhi_ready")
        hlo_ready = sem("hlo_ready")
        l1_done = sem("l1_done")
        r_ready = sem("r_ready")
        rhi_ready = sem("rhi_ready")
        rlo_ready = [sem("rlo_ready0"), sem("rlo_ready1")]
        src3_ready = sem("src3_ready")
        v2_done = sem("v2_done")
        tab_ready = sem("tab_ready")
        l2_done = sem("l2_done")
        out_ready = sem("out_ready")
        dve_stats = sem("dve_stats")
        dve_rstd = sem("dve_rstd")
        dve_top = sem("dve_top")
        dve_pre = sem("dve_pre")
        dve_acc = sem("dve_acc")
        dve_prod = sem("dve_prod")
        dve_vhi = sem("dve_vhi")
        dve_rest = sem("dve_rest")
        dve_mid = sem("dve_mid")
        dve_deg = sem("dve_deg")
        dve_group = sem("dve_group")
        pool_group = sem("pool_group")
        dve_init = sem("dve_init")

        block = ctx.enter_context(nc.Block())

        def ahead(j, last):
            return not (last and j + LEAD >= RING)

        def ahead_before(j, last):
            return not (last and j - 1 + LEAD >= RING)

        def slots(eng, slot):
            if LOOPS > 1:
                with eng.Fori(0, LOOPS, 1) as it:
                    for j in range(RING):
                        slot(it, j, False)
            else:
                for it in range(LOOPS):
                    for j in range(RING):
                        slot(it, j, False)
            for j in range(RING):
                slot(LOOPS, j, True)

        def at(it, j, per, k):
            return it * (RING * per) + (per * j + k)

        def at_group(it, j, per, k):
            return it * (RING // G * per) + (per * (j // G) + k)

        @block.sync
        def _(sp):
            sp.dma_start(xb[:, 0], x[0].rearrange("(k p) n -> p k n", p=P)).then_inc(x_loaded[0], 16)
            sp.dma_start(cst[:], small).then_inc(small_loaded, 16)
            sp.dma_start(xb[:, 1], x[1].rearrange("(k p) n -> p k n", p=P)).then_inc(x_loaded[1], 16)
            sp.dma_start(r[:].rearrange("p k n -> p (k n)")[:, 0:T_WID], staged).then_inc(consts_loaded, 16)
            sp.dma_start(w[:], w_t.rearrange("(k p) n -> p k n", p=P)).then_inc(consts_loaded, 16)
            sp.dma_start(bias1[:], b1).then_inc(consts_loaded, 16)
            sp.dma_start(bias2[:], b2).then_inc(consts_loaded, 16)
            for b in range(2, RING):
                sp.dma_start(xb[:, b], x[b].rearrange("(k p) n -> p k n", p=P)).then_inc(x_loaded[b], 16)

            x_all = x.rearrange("b (k p) n -> p b k n", p=P)
            out_all = out.rearrange("b (k p) n -> p b k n", p=P)

            def slot(it, j, last):
                b = it * RING + j
                sp.wait_ge(out_ready, at(it, j, 4, 8))
                src = xb[:, j:j + 1]
                dst = out_all[:, b:b + 1] if isinstance(b, int) else out_all[:, bass.ds(b, 1)]
                sp.dma_start(dst, src).then_inc(x_stored[j], 16)
                if not last:
                    sp.wait_ge(x_stored[j], it * 16 + 16)
                    nb = it * RING + (j + RING)
                    nxt = x_all[:, nb:nb + 1] if isinstance(nb, int) else x_all[:, bass.ds(nb, 1)]
                    sp.dma_start(xb[:, j:j + 1], nxt).then_inc(x_loaded[j], 16)

            slots(sp, slot)
            for j in range(RING):
                sp.wait_ge(x_stored[j], 16 * (NB // RING))

        @block.scalar
        def _(act):
            def root(it, j, k):
                act.wait_ge(stats_ready, at(it, j, 1, k + 1))
                nc.scalar.activation(std[:], mv[:, :, 1], ACT.Sqrt,
                                     bias=c_("eps")).then_inc(std_ready, 1)

            def normalise(it, j, k, kf):
                a = (j + k) % RING
                if kf == 0:
                    act.wait_ge(norm_ready, at(it, j, 1, k + 1))
                last = nc.scalar.activation(
                    hb[:, a, kf], xb[:, a, kf], ACT.Relu, bias=nmean[:, a % 2, kf:kf + 1],
                    scale=rstd[:, a % 2, kf:kf + 1], accum_out=h_tot[:, a, kf:kf + 1])
                if kf == KF - 1:
                    last.then_inc(h_ready, 1)

            def split_sum(it, j, k):
                act.wait_ge(hsum_ready, at(it, j, 1, k + 1))
                ago = 2 if in_first(it, j + k) else 1
                if not (in_first(it, j + k) and k < ago):
                    act.wait_ge(fv_done, at(it, j, 1, k + 1 - ago))
                whole, high, _low = sum_buffers(it, j + k)
                nc.scalar.activation(high, whole, ACT.Copy).then_inc(hshi_ready, 1)

            def take_sums(it, j, k):
                act.wait_ge(fv_done, at(it, j, 1, k + G))
                nc.scalar.activation(fv[:, 0:N], ps_fv[0:G], ACT.Copy).then_inc(fv_copied, 1)

            def split_h(it, j, k, half):
                a = (j + k) % RING
                n = slice(half * H, half * H + H)
                nc.scalar.activation(h_hi[:, :, n], hb[:, a, :, n], ACT.Copy).then_inc(hhi_ready, 1)

            def relu(it, j, half, m):
                u = 2 * half + m
                par = j % 2
                act.wait_ge(l1_done, at(it, j, 4, u + 1))
                if u == 0:
                    act.wait_ge(beta_ready, at(it, j, 1, 1))
                com = dict(bias=beta[:, par, m, 0:1], scale=1.0 / (D0 * D0))
                if half == 0:
                    nc.scalar.activation(r[:, m, K_TOP + 1:H], ps[u][:, K_TOP + 1:H], ACT.Relu,
                                         accum_out=acc[:, m, 0:1], **com)
                    nc.scalar.activation(r[:, m, 0:1], ps[u][:, 0:1], ACT.Relu,
                                         accum_out=acc[:, m, 1:2], **com)
                    last = nc.scalar.activation(
                        r[:, m, 1:K_TOP + 1], ps[u][:, 1:K_TOP + 1], ACT.Relu, bias=beta[:, par, m, 1:2],
                        scale=rdeg2[:, (j // G) % 2, j % G:j % G + 1],
                        accum_out=src2[:, par, m, C_STATIC:C_STATIC + 1])
                else:
                    last = nc.scalar.activation(r[:, m, H:N], ps[u][:], ACT.Relu,
                                                accum_out=acc[:, m, 2:3], **com)
                last.then_inc(r_ready, 1)

            def split_r(it, j, half, more):
                act.wait_ge(r_ready, at(it, j, 4, 2 * half + 2))
                if half == 1 and more:
                    act.wait_ge(sums_ready, at(it, j, 1, 2))
                n = slice(half * H, half * H + H)
                nc.scalar.activation(r_hi[:, :, n], r[:, :, n], ACT.Copy).then_inc(rhi_ready, 1)

            act.wait_ge(small_loaded, 16)
            for a in range(G + 1):
                if a == G:
                    split_sum(0, 0, G - 1)
                root(0, 0, a)
                normalise(0, 0, a, 0)
                normalise(0, 0, a, 1)
                if 0 < a < G:
                    split_sum(0, 0, a - 1)
            take_sums(0, 0, 0)
            split_h(0, 0, 0, 0)
            split_h(0, 0, 0, 1)
            split_sum(0, 0, G)

            def slot(it, j, last):
                g = j % G
                more = not (last and j == RING - 1)
                main = ahead(j, last) and g not in LATE
                late = ahead_before(j, last) and (g - 1) % G in LATE
                relu(it, j, 0, 0)
                if late:
                    root(it, j, LEAD - 1)
                elif main:
                    root(it, j, LEAD)
                relu(it, j, 0, 1)
                split_r(it, j, 0, more)
                if late:
                    normalise(it, j, LEAD - 1, 0)
                    normalise(it, j, LEAD - 1, 1)
                if g == 1 and ahead_before(j, last):
                    split_sum(it, j, LEAD - 1)
                if g == 2 and not (last and j >= G):
                    take_sums(it, j, 2)
                if main and not late:
                    normalise(it, j, LEAD, 0)
                relu(it, j, 1, 0)
                relu(it, j, 1, 1)
                split_r(it, j, 1, more)
                if main and not late:
                    normalise(it, j, LEAD, 1)
                if more:
                    split_h(it, j, 1, 0)
                if late:
                    split_sum(it, j, LEAD - 1)
                if main and late:
                    root(it, j, LEAD)
                if more:
                    split_h(it, j, 1, 1)
                if main and late:
                    normalise(it, j, LEAD, 0)
                    normalise(it, j, LEAD, 1)
                if g == 1 and main:
                    split_sum(it, j, LEAD)

            slots(act, slot)

        @block.gpsimd
        def _(pool):
            def sum_chunks(it, j, k):
                a = (j + k) % RING
                pool.wait_ge(h_ready, at(it, j, 1, k + 1))
                if not (isinstance(it, int) and it == 0 and j + k == 0):
                    pool.wait_ge(hslo_ready, at(it, j, 1, k))
                nc.gpsimd.tensor_tensor(hsum[:], hb[:, a, 0], hb[:, a, 1], ALU.add).then_inc(hsum_ready, 1)

            def split_sum(it, j, k):
                pool.wait_ge(hshi_ready, at(it, j, 1, k + 1))
                whole, high, low = sum_buffers(it, j + k)
                nc.gpsimd.tensor_tensor(low, whole, high.bitcast(F32), ALU.subtract).then_inc(hslo_ready, 1)

            def split_r(it, j, half):
                n = slice(half * H, half * H + H)
                pool.wait_ge(rhi_ready, at(it, j, 2, half + 1))
                nc.gpsimd.tensor_tensor(r_lo[:, :, n], r[:, :, n], r_hi[:, :, n].bitcast(F32),
                                        ALU.subtract).then_inc(rlo_ready[half], 1)

            def split_h(it, j, k, half):
                a = (j + k) % RING
                n = slice(half * H, half * H + H)
                pool.wait_ge(hhi_ready, at(it, j, 2, 2 * k + half + 1))
                nc.gpsimd.tensor_tensor(h_lo[:, :, n], hb[:, a, :, n], h_hi[:, :, n].bitcast(F32),
                                        ALU.subtract).then_inc(hlo_ready, 1)

            def sources(it, j, k):
                t = j + k
                a, par, gp, g = t % RING, t % 2, (t // G) % 2, t % G
                rd = rdeg[:, gp, g]
                pool.wait_ge(sums_ready, at(it, j, 1, k + 1))
                if t % G == 0:
                    pool.wait_ge(deg_ready, at_group(it, t, 1, 1))
                for c, sums in ((slice(0, 4), h_tot[:, a]), (slice(4, 8, 2), h_top[:, par]),
                                (slice(5, 8, 2), h_sta[:, par])):
                    n = len(range(*c.indices(NCLS)))
                    last = nc.gpsimd.tensor_tensor(
                        src1[:, :, c], rd[:, c].unsqueeze(1).broadcast_to([P, KF, n]),
                        sums.unsqueeze(2).broadcast_to([P, KF, n]), ALU.mult)
                last.then_inc(src1_ready, 1)

            def tables(it, j, k):
                t = j + k
                gp = (t // G) % 2
                mx = mix[:, gp]
                shape = [P, G, NCLS, NCLS]
                pool.wait_ge(deg_ready, at_group(it, t, 1, 1))
                nc.gpsimd.tensor_tensor(
                    mx[:, :, :, C_STATIC], c_("adj_static").unsqueeze(1).broadcast_to([P, G, NCLS]),
                    deg[:, :, C_STATIC].unsqueeze(2).broadcast_to([P, G, NCLS]),
                    ALU.mult).then_inc(pool_group, 1)
                nc.gpsimd.tensor_copy(mx[:, :, :, C_COMMON],
                                      c_("adj_common").unsqueeze(1).broadcast_to([P, G, NCLS])).then_inc(pool_group, 1)
                pool.wait_ge(pool_group, at_group(it, t, 3, 2))
                nc.gpsimd.tensor_tensor(
                    mx, mx, c_("keep_own").rearrange("p (c s) -> p c s", c=NCLS).unsqueeze(1).broadcast_to(shape),
                    ALU.add).then_inc(pool_group, 1)
                pool.wait_ge(pool_group, at_group(it, t, 3, 3))
                nc.gpsimd.tensor_tensor(
                    mx, mx, rdeg[:, gp].unsqueeze(3).broadcast_to(shape), ALU.mult).then_inc(mix_ready, 1)

            pool.wait_ge(consts_ready, 1)
            for a in range(G):
                split_sum(0, 0, a)
            sum_chunks(0, 0, G)
            split_h(0, 0, 0, 0)
            split_h(0, 0, 0, 1)
            split_sum(0, 0, G)
            tables(0, 0, 0)
            sources(0, 0, 0)

            def slot(it, j, last):
                g = j % G
                more = not (last and j == RING - 1)
                before = ahead_before(j, last)
                main = ahead(j, last)
                late = before and (g - 1) % G in LATE
                if g == 1 and before:
                    sum_chunks(it, j, LEAD - 1)
                split_r(it, j, 0)
                if more:
                    sources(it, j, 1)
                if late:
                    sum_chunks(it, j, LEAD - 1)
                if g == 1 and before:
                    split_sum(it, j, LEAD - 1)
                if g == 1 and main:
                    sum_chunks(it, j, LEAD)
                if more:
                    split_h(it, j, 1, 0)
                if late:
                    split_sum(it, j, LEAD - 1)
                if g == 1 and main:
                    split_sum(it, j, LEAD)
                if more:
                    split_h(it, j, 1, 1)
                if g == G - 1 and not (last and j >= G):
                    tables(it, j, 1)

            slots(pool, slot)

        @block.tensor
        def _(pe):
            def column_sums(it, j, k):
                t = j + k
                pe.wait_ge(hslo_ready, at(it, j, 1, k + 1))
                if t % G == 0 and not (isinstance(it, int) and it == 0 and t == 0):
                    pe.wait_ge(fv_copied, at_group(it, t, 1, 0))
                row = col[:, G - 1 - t % G:G - 1 - t % G + P]
                for half in range(2):
                    n = slice(half * H, half * H + H)
                    for i, part in enumerate(sum_buffers(it, t)[1:]):
                        last = nc.tensor.matmul(
                            ps_fv[:, n], row, part[:, n], start=(t % G == 0 and i == 0),
                            stop=(t % G == G - 1 and i == 1), skip_group_check=True)
                last.then_inc(fv_done, 1)

            def spread_group(it, j, k):
                t = j + k
                pe.wait_ge(code_ready, at_group(it, t, 1, 1))
                for half in range(2):
                    n = slice(half * H, half * H + H)
                    last = nc.tensor.matmul(ps_c[:, n], spread[:, G], code[:, n], start=True, stop=True)
                last.then_inc(spread_done, 1)

            def spread_counts(it, j, k):
                t = j + k
                pe.wait_ge(cntd_ready, at_group(it, t, 1, 1))
                nc.tensor.matmul(NBC, c_("ones"), cnt_d[:], start=True, stop=True).then_inc(cnt_done, 1)

            def spread_batch(it, j, k):
                t = j + k
                if t % G == 0:
                    pe.wait_ge(cnt_copied, at_group(it, t, 1, 1))
                for half in range(2):
                    n = slice(half * H, half * H + H)
                    last = nc.tensor.matmul(ps_c[:, n], spread[:, t % G], code[:, n], start=True, stop=True)
                last.then_inc(cls_done, 1)

            def class_values(it, j, k):
                pe.wait_ge(src1_ready, at(it, j, 1, k + 1))
                pe.wait_ge(sums_ready, at(it, j, 1, k + 1))
                for m in range(KF):
                    for kf in range(KF):
                        last = nc.tensor.matmul(X1[:, m], w[:, kf, m * P:m * P + P], src1[:, kf],
                                                start=(kf == 0), stop=(kf == KF - 1))
                last.then_inc(x1_done, 1)

            def product(half, hi, lo, lo_ready, between=None):
                n = slice(half * H, half * H + H)
                for part in range(2):
                    if part:
                        if between is not None:
                            between()
                        pe.wait_ge(*lo_ready)
                    for m in range(KF):
                        mm = slice(m * P, m * P + P)
                        for kf in range(KF):
                            for wt, mov in (((w_hi, lo),) if part else ((w_hi, hi), (w_lo, hi))):
                                nc.tensor.matmul(ps[2 * half + m][:], wt[:, kf, mm], mov[:, kf, n],
                                                 start=(part == 0 and kf == 0 and wt is w_hi), stop=False,
                                                 skip_group_check=True)

            def layer1(it, j, half, between=None):
                n = slice(half * H, half * H + H)
                pe.wait_ge(hhi_ready, at(it, j, 2, half + 1))
                pe.wait_ge(out_ready, at(it, j, 4, 2 * half + 2))
                product(half, h_hi, h_lo, (hlo_ready, at(it, j, 2, half + 1)), between)
                for m in range(KF):
                    nc.tensor.matmul(ps[2 * half + m][:], mask[:, j % G], onehot[:, (j // G) % 2, n],
                                     start=False, stop=True, skip_group_check=True).then_inc(l1_done, 1)

            def layer2(it, j, half, between=None):
                pe.wait_ge(rhi_ready, at(it, j, 2, half + 1))
                product(half, r_hi, r_lo, (rlo_ready[half], at(it, j, 1, 1)), between)

            def class_terms(it, j):
                pe.wait_ge(src3_ready, at(it, j, 1, 1))
                a = 96 - 32 * (j % G)
                for kf in range(KF):
                    last = nc.tensor.matmul(V2, src3[:, kf, a:a + P], w[:, kf],
                                            start=(kf == 0), stop=(kf == KF - 1))
                last.then_inc(v2_done, 1)

            def add_terms(it, j, half):
                pe.wait_ge(tab_ready, at(it, j, 1, 1))
                n = slice(half * H, half * H + H)
                for m in range(KF):
                    u = 2 * half + m
                    nc.tensor.matmul(ps[u][:], tab[:, m * P:m * P + P], onehot[:, (j // G) % 2, n],
                                     start=False, stop=True, skip_group_check=True).then_inc(l2_done, 1)

            pe.wait_ge(consts_ready, 1)
            for a in range(G):
                column_sums(0, 0, a)
            spread_group(0, 0, 0)
            spread_counts(0, 0, 0)
            spread_batch(0, 0, 0)
            class_values(0, 0, 0)

            def slot(it, j, last):
                g = j % G
                more = not (last and j == RING - 1)
                grouped = g == G - 1 and not (last and j >= G)
                before = ahead_before(j, last)

                def in_layer1():
                    if grouped:
                        spread_counts(it, j, 1)
                    if g == 2 and before:
                        column_sums(it, j, LEAD - 1)

                def in_layer2():
                    if g == 1 and before:
                        column_sums(it, j, LEAD - 1)
                    add_terms(it, j, 0)

                layer1(it, j, 0)
                if grouped:
                    spread_group(it, j, 1)
                elif more:
                    pe.wait_ge(beta_ready, at(it, j, 1, 1))
                    spread_batch(it, j, 1)
                if g in (0, 1) and not (last and j - 2 + LEAD >= RING):
                    column_sums(it, j, LEAD - 2)
                layer1(it, j, 1, in_layer1)
                if grouped:
                    spread_batch(it, j, 1)
                layer2(it, j, 0)
                if more:
                    class_values(it, j, 1)
                class_terms(it, j)
                layer2(it, j, 1, in_layer2)
                add_terms(it, j, 1)

            slots(pe, slot)

        @block.vector
        def _(dve):
            def hold(s, value):
                dve.wait_ge(s, value)
                nc.vector.memset(cell[:], 0.0)

            def moments(it, j, k):
                a = (j + k) % RING
                q = (j + k) // RING
                dve.wait_ge(x_loaded[a], it * 16 + 16 * (q + 1))
                for kf in range(KF):
                    for half in range(2):
                        last = nc.vector.bn_stats(stats[:, kf, half], xb[:, a, kf, half * H:half * H + H])
                last.then_inc(dve_stats, 1)
                hold(dve_stats, at(it, j, 1, k + 1))
                for kf in range(KF):
                    last = nc.vector.bn_aggr(mv[:, kf], stats[:, kf].rearrange("p a b -> p (a b)"))
                last.then_inc(stats_ready, 1)

            def scales(it, j, k):
                a = (j + k) % RING
                dve.wait_ge(std_ready, at(it, j, 1, k + 1))
                nc.vector.reciprocal(rstd[:, a % 2], std[:]).then_inc(dve_rstd, 1)
                dve.wait_ge(dve_rstd, at(it, j, 1, k + 1))
                nc.vector.scalar_tensor_tensor(nmean[:, a % 2], mv[:, :, 0], -1.0, rstd[:, a % 2],
                                               ALU.mult, ALU.mult).then_inc(norm_ready, 1)

            def node_sums(it, j, k):
                t = j + k
                a, par = t % RING, t % 2
                dve.wait_ge(h_ready, at(it, j, 1, k + 1))
                nc.vector.tensor_reduce(h_sta[:, par], hb[:, a, :, 1:K_TOP + 1], AX_X, ALU.add)
                dve.wait_ge(cls_done, at(it, j, 1, k + 1))
                for kf in range(KF):
                    if kf > 0:
                        dve.wait_ge(dve_top, at(it, j, 1, k + 1))
                    last = nc.vector.scalar_tensor_tensor(
                        junk, ps_c[:].rearrange("p (h n) -> p h n", h=2), 4.0,
                        hb[:, a, kf].rearrange("p (h n) -> p h n", h=2), ALU.is_lt, ALU.mult,
                        accum_out=h_top[:, par, kf:kf + 1])
                    last.then_inc(dve_top if kf == 0 else sums_ready, 1)

            def class_biases(it, j, k):
                t = j + k
                par, gp, g = t % 2, (t // G) % 2, t % G
                dve.wait_ge(x1_done, at(it, j, 1, k + 1))
                nc.vector.tensor_tensor(pre[:], X1, bias1[:].unsqueeze(2).broadcast_to([P, KF, NCLS]),
                                        ALU.add).then_inc(dve_pre, 1)
                dve.wait_ge(dve_pre, at(it, j, 1, k + 1))
                nc.vector.tensor_scalar(src2[:, par], pre[:], 0.0, None, ALU.max)
                nc.vector.tensor_tensor(
                    beta[:, par], pre[:, :, C_COMMON:NCLS:2],
                    rdeg[:, gp, g, C_COMMON:NCLS:2].unsqueeze(1).broadcast_to([P, KF, 2]),
                    ALU.mult).then_inc(beta_ready, 1)

            def split_r(it, j, half):
                n = slice(half * H, half * H + H)
                dve.wait_ge(rhi_ready, at(it, j, 2, half + 1))
                nc.vector.tensor_tensor(r_lo[:, :, n], r[:, :, n], r_hi[:, :, n].bitcast(F32),
                                        ALU.subtract).then_inc(rlo_ready[half], 1)

            def class_terms(it, j):
                par, gp, g = j % 2, (j // G) % 2, j % G
                dve.wait_ge(r_ready, at(it, j, 4, 4))
                nc.vector.tensor_reduce(src2[:, par, :, C_COMMON], acc[:], AX_X, ALU.add).then_inc(dve_acc, 1)
                if g == 0:
                    dve.wait_ge(mix_ready, at_group(it, j, 1, 1))
                dve.wait_ge(dve_acc, at(it, j, 1, 1))
                for kf in range(KF):
                    last = nc.vector.tensor_tensor(
                        prod[:, kf], src2[:, par, kf].unsqueeze(1).broadcast_to([P, NCLS, NCLS]),
                        mix[:, gp, g], ALU.mult)
                last.then_inc(dve_prod, 1)
                dve.wait_ge(dve_prod, at(it, j, 1, 1))
                for dup in range(3):
                    last = nc.vector.tensor_reduce(src3[:, :, 96 + 8 * dup:104 + 8 * dup], prod[:], AX_X, ALU.add)
                last.then_inc(src3_ready, 1)

            def table(it, j):
                dve.wait_ge(v2_done, at(it, j, 1, 1))
                nc.vector.tensor_copy(v_hi[:], V2).then_inc(dve_vhi, 1)
                dve.wait_ge(dve_vhi, at(it, j, 1, 1))
                nc.vector.scalar_tensor_tensor(v_rest[:], v_hi[:], c_("less_hi"), V2,
                                               ALU.mult, ALU.add).then_inc(dve_rest, 1)
                dve.wait_ge(dve_rest, at(it, j, 1, 1))
                nc.vector.tensor_copy(v_hi[:], v_rest[:]).then_inc(dve_mid, 1)
                dve.wait_ge(dve_mid, at(it, j, 1, 1))
                nc.vector.scalar_tensor_tensor(tab[:], v_hi[:], c_("less_mid"), v_rest[:],
                                               ALU.mult, ALU.add).then_inc(tab_ready, 1)

            def finish(it, j, half):
                n = slice(half * H, half * H + H)
                for m in range(KF):
                    u = 2 * half + m
                    dve.wait_ge(l2_done, at(it, j, 4, u + 1))
                    nc.vector.scalar_tensor_tensor(xb[:, j, m, n], ps[u][:], bias2[:, m:m + 1],
                                                   xb[:, j, m, n], ALU.add, ALU.add).then_inc(out_ready, 1)

            def top_nodes(it, j, k, part):
                t = j + k

                def link(ins, n):
                    ins.then_inc(dve_group, 1)
                    hold(dve_group, at_group(it, t, 5, n))

                if part == "best":
                    if not (isinstance(it, int) and it == 0 and t == 0):
                        dve.wait_ge(cls_done, at(it, j, 1, k))
                    nc.vector.memset(first[:], PAST)
                    nc.vector.memset(fv[:, N:], PAST)
                    hold(fv_copied, at_group(it, t, 1, 1))
                    nc.vector.max(best[:], fv[:, 0:N]).then_inc(dve_group, 1)
                elif part == "first":
                    nc.vector.tensor_scalar(code[0:G], fv[:, 0:N], 0.0, 4.0, ALU.is_equal,
                                            ALU.add).then_inc(zero_ready, 1)
                    dve.wait_ge(dve_group, at_group(it, t, 5, 1))
                    link(nc.vector.tensor_copy(first[:, 0:1], best[:, 0:1]), 2)
                    nc.vector.match_replace(fv[:], first[:], fv[:], T_MARK).then_inc(dve_group, 1)
                elif part == "static":
                    dve.wait_ge(zero_ready, at_group(it, t, 1, 1))
                    nc.vector.tensor_scalar(code[0:G, 1:K_TOP + 1], code[0:G, 1:K_TOP + 1], 2.0, None,
                                            ALU.add)
                elif part == "next 8":
                    hold(dve_group, at_group(it, t, 5, 3))
                    nc.vector.max(best[:], fv[:, 0:N]).then_inc(dve_group, 1)
                elif part == "mark":
                    hold(dve_group, at_group(it, t, 5, 4))
                    nc.vector.match_replace(fv[:, 0:N], best[:], fv[:, 0:N], M_MARK).then_inc(dve_group, 1)
                else:
                    dve.wait_ge(dve_group, at_group(it, t, 5, 5))
                    nc.vector.scalar_tensor_tensor(code[0:G], fv[:, 0:N], 0.0, code[0:G], ALU.min,
                                                   ALU.add).then_inc(code_ready, 1)

            def group_onehot(it, j, k):
                t = j + k
                gp = (t // G) % 2
                dve.wait_ge(spread_done, at_group(it, t, 1, 1))
                nc.vector.tensor_scalar(onehot[:, gp], ps_c[:], c_("cls"), None, ALU.is_equal, ALU.add,
                                        accum_out=cnt[:]).then_inc(onehot_ready, 1)
                dve.wait_ge(onehot_ready, at_group(it, t, 1, 1))
                nc.vector.tensor_scalar(cnt_d[:], c_("pick_n"), cnt[:], None, ALU.mult).then_inc(cntd_ready, 1)

            def group_degrees(it, j, k):
                t = j + k
                gp = (t // G) % 2
                shape = [P, G, NCLS, NCLS]
                dve.wait_ge(cnt_done, at_group(it, t, 1, 1))
                nc.vector.tensor_copy(cnt_b[:].rearrange("p g c -> p (g c)"), NBC).then_inc(cnt_copied, 1)
                dve.wait_ge(cnt_copied, at_group(it, t, 1, 1))
                nc.vector.tensor_tensor(
                    mix[:, gp], c_("adj").rearrange("p (c s) -> p c s", c=NCLS).unsqueeze(1).broadcast_to(shape),
                    cnt_b[:].unsqueeze(2).broadcast_to(shape), ALU.mult).then_inc(dve_deg, 1)
                dve.wait_ge(dve_deg, at_group(it, t, 3, 1))
                nc.vector.tensor_reduce(deg[:], mix[:, gp], AX_X, ALU.add).then_inc(dve_deg, 1)
                dve.wait_ge(dve_deg, at_group(it, t, 3, 2))
                nc.vector.tensor_tensor(deg[:], deg[:], c_("own").unsqueeze(1).broadcast_to([P, G, NCLS]),
                                        ALU.add).then_inc(dve_deg, 1)
                dve.wait_ge(dve_deg, at_group(it, t, 3, 3))
                nc.vector.reciprocal(rdeg[:, gp], deg[:]).then_inc(deg_ready, 1)
                dve.wait_ge(deg_ready, at_group(it, t, 1, 1))
                nc.vector.tensor_tensor(rdeg2[:, gp], rdeg[:, gp, :, C_STATIC], rdeg[:, gp, :, C_STATIC],
                                        ALU.mult)

            def first_sum(a):
                dve.wait_ge(h_ready, a + 1)
                if a > 1:
                    dve.wait_ge(hslo_ready, a - 1)
                nc.vector.tensor_tensor(sum_buffers(0, a)[0], hb[:, a, 0], hb[:, a, 1], ALU.add).then_inc(hsum_ready, 1)

            nc.vector.memset(code[:], 0.0).then_inc(zeroed, 1)
            nc.vector.memset(src3[:], 0.0).then_inc(zeroed, 1)
            moments(0, 0, 0)
            scales(0, 0, 0)
            moments(0, 0, 1)
            dve.wait_ge(small_loaded, 16)
            dve.wait_ge(consts_loaded, 16 * 4)
            flat = r[:].rearrange("p k n -> p (k n)")
            nc.vector.tensor_copy(mask[:].rearrange("p g n -> p (g n)"), flat[:, 0:G * P])
            nc.vector.tensor_copy(spread[:].rearrange("p g n -> p (g n)"), flat[:, G * P:(2 * G + 1) * P])
            nc.vector.tensor_copy(col[:], flat[:, (2 * G + 1) * P:T_WID])
            nc.vector.tensor_copy(w_hi[:], w[:]).then_inc(dve_init, 1)
            dve.wait_ge(dve_init, 1)
            nc.vector.tensor_tensor(w_lo[:], w[:], w_hi[:].bitcast(F32), ALU.subtract).then_inc(out_ready, 4)
            dve.wait_ge(out_ready, 4)
            nc.vector.memset(cell[:], 0.0).then_inc(consts_ready, 1)

            for a in range(1, G):
                if a > 1:
                    moments(0, 0, a)
                scales(0, 0, a)
                first_sum(a - 1)
            first_sum(G - 1)
            moments(0, 0, G)
            scales(0, 0, G)
            moments(0, 0, LEAD - 1)
            dve.wait_ge(stats_ready, LEAD)
            for part in ("best", "first", "static", "next 8", "mark", "code"):
                top_nodes(0, 0, 0, part)
            group_onehot(0, 0, 0)
            group_degrees(0, 0, 0)
            node_sums(0, 0, 0)
            class_biases(0, 0, 0)

            def slot(it, j, last):
                more = not (last and j == RING - 1)
                main = ahead(j, last) and j % G not in LATE
                late = ahead_before(j, last) and (j - 1) % G in LATE
                if late:
                    scales(it, j, LEAD - 1)
                elif main:
                    moments(it, j, LEAD)
                if j % G == G - 1 and not (last and j >= G):
                    group_onehot(it, j, 1)
                    group_degrees(it, j, 1)
                if more:
                    node_sums(it, j, 1)
                if main and late:
                    moments(it, j, LEAD)
                elif main:
                    scales(it, j, LEAD)
                grouping = j % G == 2 and not (last and j >= G)

                def top(part):
                    if grouping:
                        top_nodes(it, j, 2, part)

                top("best")
                class_terms(it, j)
                split_r(it, j, 1)
                top("first")
                table(it, j)
                if main and late:
                    scales(it, j, LEAD)
                if more:
                    class_biases(it, j, 1)
                top("static")
                finish(it, j, 0)
                top("next 8")
                finish(it, j, 1)
                top("mark")
                top("code")
                if ahead(j, last) and j % G in LATE:
                    moments(it, j, LEAD)

            slots(dve, slot)


def kernel(x, adj, L0_gnn_b1, L0_gnn_b2):
    import concourse.bacc as bacc
    from concourse.bass_utils import run_bass_kernel_spmd

    small, staged = constants()
    arrays = {
        "x": np.ascontiguousarray(x),
        "w_t": np.ascontiguousarray(np.asarray(adj).T),
        "b1": np.ascontiguousarray(np.asarray(L0_gnn_b1).reshape(KF, P).T),
        "b2": np.ascontiguousarray(np.asarray(L0_gnn_b2).reshape(KF, P).T),
        "small": small,
        "staged": staged,
    }
    nc = bacc.Bacc("TRN2", target_bir_lowering=False, num_devices=1)
    ins = [nc.dram_tensor(name, a.shape, F32, kind="ExternalInput").ap() for name, a in arrays.items()]
    out = nc.dram_tensor("out", arrays["x"].shape, F32, kind="ExternalOutput").ap()
    build(nc, *ins, out)
    result = run_bass_kernel_spmd(nc, [arrays], core_ids=[0])
    return result.results[0]["out"]
```
